# Optimizing a Trainium2 kernel written in Bass

```python
import numpy as np
import jax
import jax.numpy as jnp

def _softmax(x, axis=-1):
    return jax.nn.softmax(x, axis=axis)

def _gelu(x):
    return jax.nn.gelu(x, approximate=True)

def _silu(x):
    return jax.nn.silu(x)

def _sigmoid(x):
    return jax.nn.sigmoid(x)

def _layernorm(x, axis=-1, eps=1e-05):
    m = jnp.mean(x, axis=axis, keepdims=True)
    v = jnp.var(x, axis=axis, keepdims=True)
    return (x - m) / jnp.sqrt(v + eps)

def _scatter_add(tgt, idx, src, axis=0):
    return tgt.at[idx].add(src)

def _segment_sum(src, seg, n):
    return jax.ops.segment_sum(src, seg, n)
kernel_name = 'mk_flamingo_gated_d1_seqx_r4_d4fdd2'

def setup_inputs(seed: int=0):
    np.random.seed(seed)
    _w = jnp.asarray

    def _rec_inputs():
        import jax
        import jax.numpy as jnp
        _rk = jax.random.key(seed)
        x = 2.818e-05 + 1 * jax.random.normal(jax.random.fold_in(_rk, 1), (1, 2048, 256), jnp.float32)
        _lenS = 2048 - jax.random.randint(jax.random.fold_in(_rk, 7), (1,), 0, max(1, 2048 // 4) + 1, jnp.int32)
        _lenS2 = 1601 - jax.random.randint(jax.random.fold_in(_rk, 8), (1,), 0, max(1, 1601 // 4) + 1, jnp.int32)
        _ctx_1024P = jax.random.normal(jax.random.fold_in(_rk, 11), (1, 16, 256), jnp.float32)
        _ctx_1024c = jax.random.dirichlet(jax.random.fold_in(_rk, 511), 0.3 * jnp.ones((16,), jnp.float32), (1, 1601))
        _ctx_1024t = jnp.einsum('bsk,bkd->bsd', _ctx_1024c, _ctx_1024P)
        _ctx_1024t = _ctx_1024t * jax.lax.rsqrt(jnp.mean(jnp.square(_ctx_1024t)) + 1e-12) * 0.953939
        ctx_1024 = -0.000392918 + 0.999932 * (_ctx_1024t + 0.3 * jax.random.normal(jax.random.fold_in(_rk, 611), (1, 1601, 256), jnp.float32))
        _g = jax.random.normal(jax.random.fold_in(_rk, 9001), (2, 1), jnp.float32)
        _g = jnp.sign(_g) * jnp.maximum(jnp.abs(_g), 1.0) + (_g == 0) * 1.0
        g_xattn = _g[0]
        g_ffn = _g[1]
        return (x, ctx_1024, g_xattn, g_ffn)
    x, ctx_1024, g_xattn, g_ffn = _rec_inputs()

    def _L0_xattn_setup():
        import jax, jax.numpy as jnp
        import numpy as np
        key = jax.random.key(seed)
        k1, k2 = jax.random.split(key)
        B, S_ENC, S_DEC, D = (8, 512, 512, 256)
        enc_outputs = jax.random.normal(k1, (B, S_ENC, D), dtype=jnp.float32)
        dec_outputs = jax.random.normal(k2, (B, S_DEC, D), dtype=jnp.float32)
        return {'enc_outputs': enc_outputs, 'dec_outputs': dec_outputs}
    _L0_xattn_all = _L0_xattn_setup()
    _L0_xattn_in = {k: v for k, v in _L0_xattn_all.items() if k in ()}
    del _L0_xattn_all

    def _L0_ffn_setup():
        import jax, jax.numpy as jnp
        import numpy as np
        B, S, D, E, H, O = (4, 512, 256, 8, 512, 256)
        key = jax.random.key(seed)
        ks = jax.random.split(key, 8)
        sd = 1.0 / np.sqrt(D)
        sh = 1.0 / np.sqrt(H)
        return {'x': jax.random.normal(ks[0], (B, S, D), dtype=jnp.float32), 'gate_w': jax.random.uniform(ks[1], (D, E), jnp.float32, -sd, sd), 'gate_b': jax.random.uniform(ks[2], (E,), jnp.float32, -sd, sd), 'expert_w': jax.random.uniform(ks[3], (E, D, H), jnp.float32, -sd, sd), 'expert_b': jax.random.uniform(ks[4], (E, H), jnp.float32, -sd, sd), 'out_w': jax.random.uniform(ks[5], (H, O), jnp.float32, -sh, sh), 'out_b': jax.random.uniform(ks[6], (O,), jnp.float32, -sh, sh)}
    _L0_ffn_all = _L0_ffn_setup()
    _L0_ffn_in = {k: v for k, v in _L0_ffn_all.items() if k in ('gate_w', 'gate_b', 'expert_w', 'expert_b', 'out_w', 'out_b')}
    del _L0_ffn_all
    return {'x': x, 'ctx_1024': ctx_1024, 'g_xattn': g_xattn, 'g_ffn': g_ffn, 'L0_ffn_gate_w': _L0_ffn_in['gate_w'], 'L0_ffn_gate_b': _L0_ffn_in['gate_b'], 'L0_ffn_expert_w': _L0_ffn_in['expert_w'], 'L0_ffn_expert_b': _L0_ffn_in['expert_b'], 'L0_ffn_out_w': _L0_ffn_in['out_w'], 'L0_ffn_out_b': _L0_ffn_in['out_b']}

def reference(x, ctx_1024, g_xattn, g_ffn, L0_ffn_gate_w, L0_ffn_gate_b, L0_ffn_expert_w, L0_ffn_expert_b, L0_ffn_out_w, L0_ffn_out_b):
    import jax
    import jax.numpy as jnp

    def _L0_xattn_ref(enc_outputs, dec_outputs):
        import jax, jax.numpy as jnp
        import numpy as np
        a_t = jnp.einsum('bed,btd->bet', enc_outputs, dec_outputs)
        a_t = jax.nn.softmax(a_t, axis=-1)
        c_t = jnp.einsum('bet,bed->btd', a_t, enc_outputs)
        return c_t

    def _L0_ffn_ref(x, gate_w, gate_b, expert_w, expert_b, out_w, out_b):
        import jax, jax.numpy as jnp
        import numpy as np
        B, S, D, E, H, O = (4, 512, 256, 8, 512, 256)
        Bq, Sq, Dq = x.shape
        xt = x.reshape(-1, Dq)
        logits = xt @ gate_w + gate_b
        idx = jnp.argmax(logits, axis=-1)
        all_out = jnp.einsum('td,edh->teh', xt, expert_w) + expert_b[None]
        onehot = jax.nn.one_hot(idx, expert_w.shape[0], dtype=x.dtype)
        sel = jnp.einsum('te,teh->th', onehot, all_out)
        out = sel @ out_w + out_b
        return out.reshape(Bq, Sq, -1)
    x = x + jnp.tanh(g_xattn[0]) * _L0_xattn_ref(ctx_1024, _layernorm(x, axis=-1))
    x = x + jnp.tanh(g_ffn[0]) * _L0_ffn_ref(_layernorm(x, axis=-1), L0_ffn_gate_w, L0_ffn_gate_b, L0_ffn_expert_w, L0_ffn_expert_b, L0_ffn_out_w, L0_ffn_out_b)
    return x

_drawn_inputs = setup_inputs


def setup_inputs(seed=0):
    import zlib

    import numpy as np

    out = dict(_drawn_inputs(seed))
    spreads = {}
    factors = {'L0_ffn_expert_b': 6.845, 'L0_ffn_out_b': 5.484}
    for name, (base, spread) in spreads.items():
        noise = np.random.default_rng([zlib.crc32(name.encode()), seed]).standard_normal(out[name].shape)
        drawn = base * np.exp(spread * noise) if base else spread * noise
        out[name] = jnp.asarray(drawn.astype(out[name].dtype))
    for name, factor in factors.items():
        out[name] = (out[name] * factor).astype(out[name].dtype)
    return out
```

```python
from contextlib import ExitStack

import concourse.bass as bass
from concourse import mybir

ALU = mybir.AluOpType
ACT = mybir.ActivationFunctionType
F32 = mybir.dt.float32
F16 = mybir.dt.float16
AX_X = mybir.AxisListType.X

P = 128
BANK = 512

LN2 = 0.6931471805599453
PROB_SHIFT = 10 * LN2
CTX_SCALE = 2.0 ** 16
C_UNSCALE = 2.0 ** -16
W_SCALE = 2.0 ** 8
M_SCALE = 2.0 ** -8
OUT_UNSCALE = 2.0 ** -8
EPS = 1e-5


def bass_flamingo_gated_block(
    nc: bass.Bass,
    x: bass.AP,
    ctx_rows: bass.AP,
    g_xattn: bass.AP,
    g_ffn: bass.AP,
    gate_w: bass.AP,
    gate_b: bass.AP,
    expert_w: bass.AP,
    expert_b: bass.AP,
    out_w: bass.AP,
    out_b: bass.AP,
    out: bass.AP,
):
    _, T, D = x.shape
    S = ctx_rows.shape[1]
    NE, _, H = expert_w.shape
    O = out_w.shape[1]
    NT = T // P
    NS = -(-S // P)
    NF = S // P
    REST = S - NF * P
    KD = D // P
    KH = H // P
    NC = T // BANK
    NB = NE * O // BANK
    EPB = NE // NB
    WS = 3
    XG = 4
    NX = NT // XG
    assert KD == 2 and NC == 4 and NB == 4 and EPB == 2 and NS == NF + 1 and NS % 2 == 1 and D == O == 256

    def rows(j):
        return P if isinstance(j, int) is False or j < NF else REST

    with ExitStack() as stack:
        def sb(name, shape, dt):
            return stack.enter_context(nc.sbuf_tensor(name, shape, dt))

        def sem(name):
            return stack.enter_context(nc.semaphore(name))

        xt = sb("xt", [P, NT, D], F32)
        ctx = sb("ctx", [P, NS, D], F32)
        prob = sb("prob", [P, 2, T], F32)
        ynorm = prob[:, :, :].rearrange("p b (t d) -> p (b t) d", d=D)
        yT_hi = sb("yT_hi", [P, KD, T], F16)
        yT_lo = sb("yT_lo", [P, KD, T], F16)
        fold_hi, fold_lo = yT_hi, yT_lo
        cT_hi = sb("cT_hi", [P, NS, D], F16)
        cT_lo = sb("cT_lo", [P, NS, D], F16)
        ctxn_hi, ctxn_lo = cT_hi, cT_lo
        p_hi = sb("p_hi", [P, NS, T], F16)
        p_lo = sb("p_lo", [P, NS, T], F16)
        ew = sb("ew", [P, WS, KD, H], F32)
        ow_hi = sb("ow_hi", [P, KH, O], F16)
        ow_lo = sb("ow_lo", [P, KH, O], F16)
        area = sb("area", [P, KH * O], F32)
        ow = area[:, :].rearrange("p (c o) -> p c o", c=KH)
        wT = area[:, :].bitcast(F16).rearrange("p (b s c d) -> p b s c d", b=2, s=2, c=KH)
        y2 = area[:, 0:2 * D].rearrange("p (b d) -> p b d", b=2)
        y2T = area[:, 2 * D:4 * D].bitcast(F16).rearrange("p (b s k t) -> p b s k t", b=2, s=2, k=KD)
        eb = sb("eb", [64, H], F32)
        ebT_hi = sb("ebT_hi", [P, KH, 64], F16)
        ebT_lo = sb("ebT_lo", [P, KH, 64], F16)
        bias_f = sb("bias_f", [64, O], F32)
        ob = sb("ob", [64, O], F32)
        bias2 = sb("bias2", [64, O], F16)
        gw = sb("gw", [P, KD, NE], F32)
        gw_hi = sb("gw_hi", [P, KD, NE], F16)
        gw_lo = sb("gw_lo", [P, KD, NE], F16)
        gb = sb("gb", [P, NE], F32)
        gates = sb("gates", [P, 2], F32)
        tgates = sb("tgates", [P, 2], F32)
        gscale = sb("gscale", [P, 3], F32)
        ctxn = sb("ctxn", [P, D], F32)
        ident = sb("ident", [P, P], F32)
        ident16 = sb("ident16", [P, P], F16)
        desc = sb("desc", [P, NE], F32)
        held = sb("held", [P, 1], F32)
        eps = sb("eps", [P, 1], F32)
        stat6 = sb("stat6", [P, NT, 6], F32)
        stat2 = sb("stat2", [P, NT, 2], F32)
        sd = sb("sd", [P, NT], F32)
        rs = sb("rs", [P, NT], F32)
        nmr = sb("nmr", [P, NT], F32)
        smax = sb("smax", [P, NS], F32)
        nbias = sb("nbias", [P, NS], F32)
        zsum = sb("zsum", [P, NS], F32)
        rz = sb("rz", [P, NS], F32)
        bstat6 = sb("bstat6", [P, 2, 6], F32)
        bstat2 = sb("bstat2", [P, 2, 2], F32)
        bsd = sb("bsd", [P, 2], F32)
        brs = sb("brs", [P, 2], F32)
        bnmr = sb("bnmr", [P, 2], F32)
        lg = sb("lg", [P, NE], F32)
        lmax = sb("lmax", [P, 1], F32)
        wsel = sb("wsel", [P, NE], F32)
        wmax = sb("wmax", [P, 1], F32)
        mask = sb("mask", [P, NE], F32)
        onehot = sb("onehot", [P, P], F16)
        onehotT = sb("onehotT", [P, P], F16)

        ps = stack.enter_context(nc.psum_tensor("ps", [P, 8, BANK], F32))
        ps16 = ps[:, 7, 256:384].bitcast(F16)
        C_BANK, FFN_BANK, T_BANK, G_BANK = 0, 2, 6, 7
        logits_ps = ps[:, G_BANK, 0:NE]
        bias_ps = ps[:, G_BANK, 0:O]

        x_loaded = [sem(f"x_loaded{g}") for g in range(NX)]
        ctx_loaded = [sem(f"ctx_loaded{g}") for g in range(4)]
        small_loaded = sem("small_loaded")
        bias_loaded = sem("bias_loaded")
        ow_loaded = sem("ow_loaded")
        ew_loaded = [sem(f"ew_loaded{s}") for s in range(WS)]
        out_stored = sem("out_stored")
        ident_zeroed = sem("ident_zeroed")
        consts_ready = sem("consts_ready")
        gate_zeroed = sem("gate_zeroed")
        stat6_done = sem("stat6_done")
        stat2_done = sem("stat2_done")
        sd_ready = sem("sd_ready")
        rs_done = sem("rs_done")
        nmr_done = sem("nmr_done")
        y_ready = sem("y_ready")
        tr_ready = sem("tr_ready")
        tr_hi_done = sem("tr_hi_done")
        tr_lo_done = sem("tr_lo_done")
        tanh_done = sem("tanh_done")
        gscale_ready = sem("gscale_ready")
        scores_ready = sem("scores_ready")
        smax_done = sem("smax_done")
        nbias_ready = sem("nbias_ready")
        exp_done = sem("exp_done")
        p_hi_ready = sem("p_hi_ready")
        p_lo_ready = sem("p_lo_ready")
        rz_ready = sem("rz_ready")
        ctxn_done = sem("ctxn_done")
        ctxn_hi_done = sem("ctxn_hi_done")
        ctxn_ready = sem("ctxn_ready")
        ow_scaled = sem("ow_scaled")
        ow_hi_done = sem("ow_hi_done")
        small_ready = sem("small_ready")
        ebT_ready = sem("ebT_ready")
        ebT_hi_done = sem("ebT_hi_done")
        ebT_lo_done = sem("ebT_lo_done")
        bias_acc = sem("bias_acc")
        bias_step = sem("bias_step")
        wT_ready = sem("wT_ready")
        wT_hi_done = sem("wT_hi_done")
        wT_lo_done = sem("wT_lo_done")
        fold_ready = sem("fold_ready")
        fold_hi_done = sem("fold_hi_done")
        fold_lo_done = sem("fold_lo_done")
        c_ready = sem("c_ready")
        x1_done = sem("x1_done")
        b6_done = sem("b6_done")
        b2_done = sem("b2_done")
        bsd_ready = sem("bsd_ready")
        brs_done = sem("brs_done")
        bnmr_ready = sem("bnmr_ready")
        y2_ready = sem("y2_ready")
        y2T_ready = sem("y2T_ready")
        y2T_hi_done = sem("y2T_hi_done")
        y2T_lo_done = sem("y2T_lo_done")
        logits_ready = sem("logits_ready")
        lg_done = sem("lg_done")
        lmax_done = sem("lmax_done")
        wsel_done = sem("wsel_done")
        wmax_done = sem("wmax_done")
        mask_done = sem("mask_done")
        onehot_ready = sem("onehot_ready")
        onehotT_ready = sem("onehotT_ready")
        onehotT_done = sem("onehotT_done")
        bias_ready = sem("bias_ready")
        bank_ready = sem("bank_ready")
        acc_done = sem("acc_done")

        x_view = x.rearrange("a (p i) d -> p (a i) d", i=NT)
        out_view = out.rearrange("a (p i) d -> p (a i) d", i=NT)
        ctx_full = ctx_rows[:, 0:NF * P, :].rearrange("a (p j) d -> p (a j) d", j=NF)
        ctx_rest = ctx_rows[0, NF * P:S, :]
        CG = NF // 3

        NCG = (NS + 1) // 2
        order = [("c", 0)]
        for c in range(NC):
            order += [("x", 2 * c), ("x", 2 * c + 1), ("c", c + 1)]
            if c:
                order.append(("s", c - 1))
        order += [("s", NC - 1)] + [("c", g) for g in range(NC + 1, NCG)]
        groups = [g for g in order if g[0] != "s"]
        NG = len(groups)
        TR_RING = 4

        def group_io(n):
            kind, g = groups[n]
            bank = ps[:, 4 + n % TR_RING, :]
            if kind == "x":
                src = bank.rearrange("p (k c) -> p k c", k=KD)
                return src, [t[:, :, 2 * g * P:2 * (g + 1) * P] for t in (yT_hi, yT_lo)]
            if g < NCG - 1:
                src = bank.rearrange("p (j c) -> p j c", j=2)
                return src, [t[:, 2 * g:2 * g + 2, :] for t in (cT_hi, cT_lo)]
            src = bank[:, 0:D].rearrange("p (k c) -> p k c", k=KD)[:, :, 0:REST]
            return src, [t[:, NS - 1, :].rearrange("p (k c) -> p k c", k=KD)[:, :, 0:REST] for t in (cT_hi, cT_lo)]

        block = stack.enter_context(nc.Block())

        @block.sync
        def _(sp):
            for g in range(NX):
                sp.dma_start(xt[:, XG * g:XG * (g + 1), :], x_view[:, XG * g:XG * (g + 1), :]).then_inc(x_loaded[g], 16)
            sp.dma_start(gates[:, 0:1], g_xattn.rearrange("(a b) -> a b", a=1).broadcast_to([P, 1])).then_inc(small_loaded, 16)
            sp.dma_start(gates[:, 1:2], g_ffn.rearrange("(a b) -> a b", a=1).broadcast_to([P, 1])).then_inc(small_loaded, 16)
            sp.dma_start(gw[:, :, :], gate_w.rearrange("(k p) e -> p k e", p=P)).then_inc(small_loaded, 16)
            sp.dma_start(gb[:, :], gate_b.rearrange("(a e) -> a e", a=1).broadcast_to([P, NE])).then_inc(small_loaded, 16)
            sp.dma_start(ow, out_w.rearrange("(c p) o -> p c o", p=P)).then_inc(ow_loaded, 16)
            sp.dma_start(ob[:, :], out_b.rearrange("(a o) -> a o", a=1).broadcast_to([64, O])).then_inc(bias_loaded, 16)
            sp.wait_ge(gate_zeroed, 1)
            sp.dma_start(eb[0:NE, :], expert_b).then_inc(bias_loaded, 16)
            sp.dma_start(eb[32:32 + NE, :], expert_b).then_inc(bias_loaded, 16)
            for e in range(NE):
                if e >= WS:
                    sp.wait_ge(wT_ready, KD * (e - WS + 1))
                sp.dma_start(ew[:, e % WS, :, :], expert_w[e].rearrange("(k p) h -> p k h", p=P)).then_inc(ew_loaded[e % WS], 16)
            with sp.Fori(0, NT) as i:
                sp.wait_ge(acc_done, (NE + 1) * i + (NE + 1))
                sp.dma_start(out_view[:, bass.ds(i, 1), :], xt[:, bass.ds(i, 1), :]).then_inc(out_stored, 16)
            sp.wait_ge(out_stored, 16 * NT)

        @block.gpsimd
        def _(pool):
            nc.gpsimd.memset(ident[:, :], 0.0).then_inc(ident_zeroed, 1)
            pool.wait_ge(ident_zeroed, 1)
            nc.gpsimd.affine_select(out=ident[:, :], in_=ident[:, :], compare_op=ALU.not_equal, fill=1.0,
                                    base=0, pattern=[[-1, P]], channel_multiplier=1).then_inc(consts_ready, 1)
            nc.gpsimd.memset(eps[:, :], EPS).then_inc(consts_ready, 1)
            nc.gpsimd.memset(eb[:, :], 0.0).then_inc(gate_zeroed, 1)
            nc.gpsimd.memset(bias2[:, :], 0.0).then_inc(consts_ready, 1)
            nc.gpsimd.memset(onehot[:, :], 0.0).then_inc(consts_ready, 1)
            for e in range(NE):
                nc.gpsimd.memset(desc[:, e:e + 1], float(NE - e)).then_inc(consts_ready, 1)
            pool.wait_ge(consts_ready, 1)
            nc.gpsimd.tensor_copy(ident16[:, :], ident[:, :]).then_inc(consts_ready, 1)
            pool.wait_ge(small_loaded, 64)
            nc.gpsimd.tensor_scalar(gw[:, :, :], gw[:, :, :], W_SCALE, None, ALU.mult).then_inc(ow_scaled, 1)
            nc.gpsimd.tensor_scalar(gb[:, :], gb[:, :], W_SCALE, None, ALU.mult).then_inc(small_ready, 1)
            pool.wait_ge(ow_loaded, 16)
            nc.gpsimd.tensor_scalar(ow, ow, W_SCALE, None, ALU.mult).then_inc(ow_scaled, 1)
            pool.wait_ge(ow_scaled, 2)
            nc.gpsimd.tensor_copy(gw_hi[:, :, :], gw[:, :, :]).then_inc(ow_hi_done, 1)
            nc.gpsimd.tensor_copy(ow_hi[:, :, :], ow).then_inc(ow_hi_done, 1)
            pool.wait_ge(ow_hi_done, 2)
            nc.gpsimd.tensor_tensor(gw_lo[:, :, :], gw[:, :, :], gw_hi[:, :, :], ALU.subtract).then_inc(small_ready, 1)
            nc.gpsimd.tensor_tensor(ow_lo[:, :, :], ow, ow_hi[:, :, :], ALU.subtract).then_inc(small_ready, 1)

            def normalise_context(j, r):
                hi = ctxn_hi[0:r, bass.ds(j, 1), :].rearrange("p a d -> p (a d)")
                lo = ctxn_lo[0:r, bass.ds(j, 1), :].rearrange("p a d -> p (a d)")
                pool.wait_ge(ctxn_done, j + 1)
                nc.gpsimd.tensor_copy(hi, ctxn[0:r, :]).then_inc(ctxn_hi_done, 1)
                pool.wait_ge(ctxn_hi_done, j + 1)
                nc.gpsimd.tensor_tensor(lo, ctxn[0:r, :], hi, ALU.subtract).then_inc(ctxn_ready, 1)

            with pool.Fori(0, NF) as j:
                normalise_context(j, P)
            normalise_context(NF, REST)

        @block.scalar
        def _(act):
            for g in range(3):
                act.dma_start(ctx[:, CG * g:CG * (g + 1), :], ctx_full[:, CG * g:CG * (g + 1), :]).then_inc(ctx_loaded[g], 16)
            act.dma_start(ctx[0:REST, NF, :], ctx_rest).then_inc(ctx_loaded[3], 16)
            act.wait_ge(consts_ready, 2)

            def root(g):
                act.wait_ge(stat2_done, XG * (g + 1))
                nc.scalar.activation(sd[:, XG * g:XG * (g + 1)], stat2[:, XG * g:XG * (g + 1), 1], ACT.Sqrt,
                                     bias=eps[:, 0:1]).then_inc(sd_ready, 1)

            root(0)
            nx = 0
            for n, (kind, g) in enumerate(groups):
                src, (hi, _) = group_io(n)
                act.wait_ge(tr_ready, n + 1)
                nc.scalar.activation(hi, src, ACT.Copy).then_inc(tr_hi_done, 1)
                if kind == "c" and 0 <= g < NX - 1:
                    root(g + 1)
            act.wait_ge(small_loaded, 64)
            nc.scalar.activation(tgates[:, :], gates[:, :], ACT.Tanh).then_inc(tanh_done, 1)

            def softmax(j, b, r, first=False):
                act.wait_ge(nbias_ready, j + 1)
                if not first:
                    act.wait_ge(p_lo_ready, j - 1)
                nc.scalar.activation(prob[0:r, b, :], ps[0:r, 4 * b:4 * b + 4, :].rearrange("p a c -> p (a c)"), ACT.Exp,
                                     bias=nbias[0:r, bass.ds(j, 1)], accum_out=zsum[0:r, bass.ds(j, 1)]).then_inc(exp_done, 1)
                act.wait_ge(exp_done, j + 1)
                nc.scalar.activation(p_hi[0:r, bass.ds(j, 1), :].rearrange("p a t -> p (a t)"), prob[0:r, b, :],
                                     ACT.Copy).then_inc(p_hi_ready, 1)

            softmax(0, 0, P, first=True)
            softmax(1, 1, P, first=True)
            with act.Fori(1, NF // 2) as h:
                j = 2 * h
                softmax(j, 0, P)
                softmax(j + 1, 1, P)
            softmax(NF, 0, REST)

            act.wait_ge(ebT_ready, 1)
            nc.scalar.activation(ebT_hi[:, :, :], ps[:, 6, 0:KH * 64].rearrange("p (c e) -> p c e", c=KH), ACT.Copy,
                                 scale=W_SCALE).then_inc(ebT_hi_done, 1)

            def weight_hi(n, b):
                act.wait_ge(wT_ready, n + 1)
                if not (isinstance(n, int) and n < 2):
                    act.wait_ge(fold_ready, n - 1)
                nc.scalar.activation(wT[:, b, 0, :, :], ps[:, 4 + b, :].rearrange("p (c d) -> p c d", c=KH), ACT.Copy,
                                     scale=W_SCALE).then_inc(wT_hi_done, 1)

            def fold_hi_copy(n, b, e, k):
                act.wait_ge(fold_ready, n + 1)
                nc.scalar.activation(fold_hi[:, k, bass.ds(e * O, O)], ps[:, 6 + b, 0:O], ACT.Copy,
                                     scale=gscale[:, 1:2]).then_inc(fold_hi_done, 1)

            weight_hi(0, 0)
            weight_hi(1, 1)
            fold_hi_copy(0, 0, 0, 0)
            with act.Fori(1, NE) as e:
                weight_hi(2 * e, 0)
                fold_hi_copy(2 * e - 1, 1, e - 1, 1)
                weight_hi(2 * e + 1, 1)
                fold_hi_copy(2 * e, 0, e, 0)
            fold_hi_copy(2 * NE - 1, 1, NE - 1, 1)

            def onehot_out(i):
                act.wait_ge(onehotT_ready, i + 1)
                nc.scalar.activation(onehotT[:, :], ps16[:, 0:P], ACT.Copy).then_inc(onehotT_done, 1)

            def y2T_out(i, b):
                act.wait_ge(y2T_ready, i + 1)
                if not (isinstance(i, int) and i < 2):
                    act.wait_ge(bank_ready, NB * (i - 1))
                nc.scalar.activation(y2T[:, b, 0, :, :], ps[:, T_BANK, 0:D].rearrange("p (k t) -> p k t", k=KD),
                                     ACT.Copy).then_inc(y2T_hi_done, 1)

            def norm2(i, b):
                act.wait_ge(b2_done, i + 1)
                nc.scalar.activation(bsd[:, b:b + 1], bstat2[:, b, 1:2], ACT.Sqrt, bias=eps[:, 0:1]).then_inc(bsd_ready, 1)
                act.wait_ge(bnmr_ready, i + 1)
                if not (isinstance(i, int) and i < 2):
                    act.wait_ge(y2T_ready, i - 1)
                nc.scalar.activation(y2[:, b, :], xt[:, bass.ds(i, 1), :].rearrange("p a d -> p (a d)"), ACT.Identity,
                                     bias=bnmr[:, b:b + 1], scale=brs[:, b:b + 1]).then_inc(y2_ready, 1)

            act.wait_ge(fold_ready, 2 * NE)
            norm2(0, 0)
            y2T_out(0, 0)
            norm2(1, 1)
            with act.Fori(1, NT // 2) as h:
                s = 2 * h
                for u in range(2):
                    onehot_out(s + u - 2)
                    y2T_out(s + u - 1, 1 - u)
                    norm2(s + u, u)
            onehot_out(NT - 2)
            y2T_out(NT - 1, 1)
            onehot_out(NT - 1)

        @block.vector
        def _(dve):
            def statistics(g):
                dve.wait_ge(x_loaded[g], 16)
                for i in range(XG * g, XG * (g + 1)):
                    nc.vector.bn_stats(stat6[:, i, :], xt[:, i, :]).then_inc(stat6_done, 1)
                dve.wait_ge(stat6_done, XG * (g + 1))
                for i in range(XG * g, XG * (g + 1)):
                    nc.vector.bn_aggr(stat2[:, i, :], stat6[:, i, :]).then_inc(stat2_done, 1)

            def normalise(g):
                w = slice(XG * g, XG * (g + 1))
                dve.wait_ge(sd_ready, g + 1)
                nc.vector.reciprocal(rs[:, w], sd[:, w]).then_inc(rs_done, 1)
                dve.wait_ge(rs_done, g + 1)
                nc.vector.scalar_tensor_tensor(out=nmr[:, w], in0=stat2[:, w, 0], scalar=-1.0, in1=rs[:, w],
                                               op0=ALU.mult, op1=ALU.mult).then_inc(nmr_done, 1)
                dve.wait_ge(nmr_done, g + 1)
                for i in range(XG * g, XG * (g + 1)):
                    nc.vector.tensor_scalar(ynorm[:, i, :], xt[:, i, :], rs[:, i:i + 1], nmr[:, i:i + 1],
                                            ALU.mult, ALU.add).then_inc(y_ready, 1)

            statistics(0)
            normalise(0)
            for n, (kind, g) in enumerate(groups):
                if kind == "c" and g < NX - 1:
                    statistics(g + 1)
                src, (hi, lo) = group_io(n)
                dve.wait_ge(tr_hi_done, n + 1)
                nc.vector.tensor_tensor(lo, src, hi, ALU.subtract).then_inc(tr_lo_done, 1)
                if kind == "c" and g < NX - 1:
                    normalise(g + 1)

            dve.wait_ge(tanh_done, 1)
            for n, (col, scale) in enumerate(((0, CTX_SCALE), (1, M_SCALE), (1, W_SCALE))):
                nc.vector.tensor_scalar(gscale[:, n:n + 1], tgates[:, col:col + 1], scale, None, ALU.mult).then_inc(gscale_ready, 1)

            def row_max(j, b, r):
                dve.wait_ge(scores_ready, j + 1)
                c = bass.ds(j, 1)
                nc.vector.tensor_reduce(smax[0:r, c], ps[0:r, 4 * b:4 * b + 4, :].rearrange("p a c -> p (a c)"), AX_X,
                                        ALU.max).then_inc(smax_done, 1)
                dve.wait_ge(smax_done, j + 1)
                nc.vector.tensor_scalar(nbias[0:r, c], smax[0:r, c], -1.0, PROB_SHIFT, ALU.mult, ALU.add).then_inc(nbias_ready, 1)

            def split_prob(j, b, r):
                c = bass.ds(j, 1)
                dve.wait_ge(exp_done, j + 1)
                nc.vector.reciprocal(rz[0:r, c], zsum[0:r, c]).then_inc(rz_ready, 1)
                dve.wait_ge(rz_ready, j + 1)
                if not (isinstance(j, int) and j < 1):
                    dve.wait_ge(ctxn_ready, j)
                nc.vector.tensor_scalar(ctxn[0:r, :], ctx[0:r, c, :].rearrange("p a d -> p (a d)"), rz[0:r, c],
                                        gscale[0:r, 0:1], ALU.mult, ALU.mult).then_inc(ctxn_done, 1)
                dve.wait_ge(p_hi_ready, j + 1)
                nc.vector.tensor_tensor(p_lo[0:r, c, :].rearrange("p a t -> p (a t)"), prob[0:r, b, :],
                                        p_hi[0:r, c, :].rearrange("p a t -> p (a t)"), ALU.subtract).then_inc(p_lo_ready, 1)

            row_max(0, 0, P)
            row_max(1, 1, P)
            split_prob(0, 0, P)
            with dve.Fori(1, NF // 2) as h:
                j = 2 * h
                row_max(j, 0, P)
                split_prob(j - 1, 1, P)
                row_max(j + 1, 1, P)
                split_prob(j, 0, P)
            row_max(NF, 0, REST)
            split_prob(NF - 1, 1, P)
            split_prob(NF, 0, REST)

            dve.wait_ge(ebT_hi_done, 1)
            nc.vector.scalar_tensor_tensor(out=ebT_lo[:, :, :], in0=ps[:, 6, 0:KH * 64].rearrange("p (c e) -> p c e", c=KH),
                                           scalar=W_SCALE, in1=ebT_hi[:, :, :], op0=ALU.mult,
                                           op1=ALU.subtract).then_inc(ebT_lo_done, 1)

            def weight_lo(n, b):
                dve.wait_ge(wT_hi_done, n + 1)
                nc.vector.scalar_tensor_tensor(out=wT[:, b, 1, :, :], in0=ps[:, 4 + b, :].rearrange("p (c d) -> p c d", c=KH),
                                               scalar=W_SCALE, in1=wT[:, b, 0, :, :], op0=ALU.mult,
                                               op1=ALU.subtract).then_inc(wT_lo_done, 1)

            def fold_lo_part(n, b, e, k):
                dve.wait_ge(fold_hi_done, n + 1)
                w = bass.ds(e * O, O)
                nc.vector.scalar_tensor_tensor(out=fold_lo[:, k, w], in0=ps[:, 6 + b, 0:O], scalar=gscale[:, 1:2],
                                               in1=fold_hi[:, k, w], op0=ALU.mult, op1=ALU.subtract).then_inc(fold_lo_done, 1)

            weight_lo(0, 0)
            dve.wait_ge(bias_acc, 1)
            dve.wait_ge(bias_loaded, 48)
            nc.vector.scalar_tensor_tensor(out=bias_f[:, :], in0=ps[0:64, 7, 0:O], scalar=C_UNSCALE, in1=ob[:, :],
                                           op0=ALU.mult, op1=ALU.add).then_inc(bias_step, 1)
            dve.wait_ge(bias_step, 1)
            nc.vector.tensor_scalar(bias_f[:, :], bias_f[:, :], gscale[0:64, 2:3], None, ALU.mult).then_inc(bias_step, 1)
            dve.wait_ge(bias_step, 2)
            dve.wait_ge(consts_ready, 3)
            nc.vector.tensor_copy(bias2[0:NE, :], bias_f[0:NE, :]).then_inc(bias_step, 1)
            nc.vector.tensor_copy(bias2[32:32 + NE, :], bias_f[32:32 + NE, :]).then_inc(bias_step, 1)
            dve.wait_ge(bias_step, 4)
            nc.vector.tensor_tensor(bias2[32:32 + NE, :], bias_f[32:32 + NE, :], bias2[32:32 + NE, :],
                                    ALU.subtract).then_inc(bias_step, 1)
            weight_lo(1, 1)
            fold_lo_part(0, 0, 0, 0)
            with dve.Fori(1, NE) as e:
                weight_lo(2 * e, 0)
                fold_lo_part(2 * e - 1, 1, e - 1, 1)
                weight_lo(2 * e + 1, 1)
                fold_lo_part(2 * e, 0, e, 0)
            fold_lo_part(2 * NE - 1, 1, NE - 1, 1)

            def xtile(i):
                return xt[:, bass.ds(i, 1), :].rearrange("p a d -> p (a d)")

            def choose(i):
                dve.wait_ge(logits_ready, i + 1)
                nc.vector.tensor_tensor(lg[:, :], logits_ps, gb[:, :], ALU.add).then_inc(lg_done, 1)
                dve.wait_ge(lg_done, i + 1)
                nc.vector.tensor_reduce(lmax[:, :], lg[:, :], AX_X, ALU.max).then_inc(lmax_done, 1)
                dve.wait_ge(lmax_done, i + 1)
                nc.vector.scalar_tensor_tensor(out=wsel[:, :], in0=lg[:, :], scalar=lmax[:, 0:1], in1=desc[:, :],
                                               op0=ALU.is_equal, op1=ALU.mult).then_inc(wsel_done, 1)
                dve.wait_ge(wsel_done, i + 1)
                nc.vector.tensor_reduce(wmax[:, :], wsel[:, :], AX_X, ALU.max).then_inc(wmax_done, 1)
                dve.wait_ge(wmax_done, i + 1)
                if not (isinstance(i, int) and i < 1):
                    dve.wait_ge(onehotT_ready, i)
                for h in range(2):
                    ins = nc.vector.tensor_scalar(onehot[:, 32 * h:32 * h + NE], wsel[:, :], wmax[:, 0:1], None, ALU.is_equal)
                ins.then_inc(onehot_ready, 1)
                nc.vector.tensor_scalar(mask[:, :], wsel[:, :], wmax[:, 0:1], OUT_UNSCALE, ALU.is_equal,
                                        ALU.mult).then_inc(mask_done, 1)

            def residual(i, b):
                dve.wait_ge(c_ready, i + 1)
                nc.vector.scalar_tensor_tensor(out=xtile(i), in0=ps[:, C_BANK + b, 0:D], scalar=C_UNSCALE, in1=xtile(i),
                                               op0=ALU.mult, op1=ALU.add).then_inc(x1_done, 1)
                dve.wait_ge(x1_done, i + 1)
                nc.vector.memset(held[:, :], 0.0)
                nc.vector.bn_stats(bstat6[:, b, :], xtile(i)).then_inc(b6_done, 1)
                dve.wait_ge(b6_done, i + 1)
                nc.vector.memset(held[:, :], 0.0)
                nc.vector.bn_aggr(bstat2[:, b, :], bstat6[:, b, :]).then_inc(b2_done, 1)
                dve.wait_ge(bsd_ready, i + 1)
                nc.vector.reciprocal(brs[:, b:b + 1], bsd[:, b:b + 1]).then_inc(brs_done, 1)
                dve.wait_ge(brs_done, i + 1)
                nc.vector.scalar_tensor_tensor(out=bnmr[:, b:b + 1], in0=bstat2[:, b, 0:1], scalar=-1.0,
                                               in1=brs[:, b:b + 1], op0=ALU.mult, op1=ALU.mult).then_inc(bnmr_ready, 1)

            def y2T_low(i, b):
                dve.wait_ge(y2T_hi_done, i + 1)
                nc.vector.tensor_tensor(y2T[:, b, 1, :, :], ps[:, T_BANK, 0:D].rearrange("p (k t) -> p k t", k=KD),
                                        y2T[:, b, 0, :, :], ALU.subtract).then_inc(y2T_lo_done, 1)

            def combine(i):
                dve.wait_ge(bias_ready, i + 1)
                dve.wait_ge(y2_ready, i + 1)
                nc.vector.scalar_tensor_tensor(out=xtile(i), in0=bias_ps, scalar=OUT_UNSCALE, in1=xtile(i),
                                               op0=ALU.mult, op1=ALU.add).then_inc(acc_done, 1)
                dve.wait_ge(mask_done, i + 1)
                for e in range(NE):
                    if e % EPB == 0:
                        dve.wait_ge(bank_ready, NB * i + e // EPB + 1)
                    dve.wait_ge(acc_done, (NE + 1) * i + e + 1)
                    nc.vector.scalar_tensor_tensor(out=xtile(i), in0=ps[:, FFN_BANK + e // EPB, (e % EPB) * O:(e % EPB + 1) * O],
                                                   scalar=mask[:, e:e + 1], in1=xtile(i),
                                                   op0=ALU.mult, op1=ALU.add).then_inc(acc_done, 1)

            dve.wait_ge(small_ready, 3)
            dve.wait_ge(consts_ready, 13)
            residual(0, 0)
            y2T_low(0, 0)
            residual(1, 1)
            with dve.Fori(1, NT // 2) as h:
                s = 2 * h
                for u in range(2):
                    choose(s + u - 2)
                    y2T_low(s + u - 1, 1 - u)
                    residual(s + u, u)
                    combine(s + u - 2)
            choose(NT - 2)
            y2T_low(NT - 1, 1)
            combine(NT - 2)
            choose(NT - 1)
            combine(NT - 1)

        @block.tensor
        def _(pe):
            def transposes(n):
                kind, g = groups[n]
                bank = ps[:, 4 + n % TR_RING, :]
                if n >= TR_RING:
                    pe.wait_ge(tr_hi_done, n - TR_RING + 1)
                    pe.wait_ge(tr_lo_done, n - TR_RING + 1)
                if kind == "x":
                    pe.wait_ge(y_ready, 2 * g + 2)
                    for k in range(KD):
                        for h in range(2):
                            ins = nc.tensor.transpose(bank[:, (2 * k + h) * P:(2 * k + h + 1) * P],
                                                      ynorm[:, 2 * g + h, k * P:(k + 1) * P], ident[:, :])
                else:
                    last = g == NCG - 1
                    pe.wait_ge(ctx_loaded[3 if last else (2 * g + 1) // CG], 16)
                    pe.wait_ge(ctx_loaded[3 if last else 2 * g // CG], 16)
                    r = REST if last else P
                    for h in range(1 if last else 2):
                        for k in range(KD):
                            c = (2 * h + k) * P
                            ins = nc.tensor.transpose(bank[:, c:c + r], ctx[0:r, 2 * g + h, k * P:(k + 1) * P], ident[0:r, 0:r])
                ins.then_inc(tr_ready, 1)

            def score_products(j, b, r, chunks):
                for k in range(KD):
                    for part, others in ((cT_hi, (yT_hi, yT_lo)), (cT_lo, (yT_hi,))):
                        w = part[:, bass.ds(j, 1), :].rearrange("p a d -> p (a d)")[:, k * P:k * P + r]
                        for other in others:
                            for c in chunks:
                                first = k == 0 and part is cT_hi and other is yT_hi
                                last = k == KD - 1 and part is cT_lo
                                ins = nc.tensor.matmul(ps[0:r, 4 * b + c, :], w, other[:, k, c * BANK:(c + 1) * BANK],
                                                       start=first, stop=last)
                return ins

            def scores(j, b, r):
                if not (isinstance(j, int) and j < 2):
                    pe.wait_ge(exp_done, j - 1)
                score_products(j, b, r, range(NC)).then_inc(scores_ready, 1)

            pe.wait_ge(consts_ready, 1)
            n = 0
            for kind, g in order:
                if kind != "s":
                    transposes(n)
                    n += 1
                    continue
                need = groups.index(("x", 2 * g + 1)) + 1
                pe.wait_ge(tr_hi_done, need)
                pe.wait_ge(tr_lo_done, need)
                ins = score_products(0, 0, P, [g])
                if g == NC - 1:
                    ins.then_inc(scores_ready, 1)
            pe.wait_ge(tr_hi_done, NG)
            pe.wait_ge(tr_lo_done, NG)
            scores(1, 1, P)
            with pe.Fori(1, NF // 2) as h:
                j = 2 * h
                scores(j, 0, P)
                scores(j + 1, 1, P)
            scores(NF, 0, REST)

            pe.wait_ge(exp_done, NF)
            pe.wait_ge(bias_loaded, 48)
            for c in range(KH):
                ins = nc.tensor.transpose(ps[:, 6, 64 * c:64 * (c + 1)], eb[:, c * P:(c + 1) * P], ident[0:64, 0:64])
            ins.then_inc(ebT_ready, 1)

            def weight_transposes(n, b, slot, k):
                if not (isinstance(n, int) and n < 2):
                    pe.wait_ge(wT_lo_done, n - 1)
                for c in range(KH):
                    ins = nc.tensor.transpose(ps[:, 4 + b, c * P:(c + 1) * P], ew[:, slot, k, c * P:(c + 1) * P], ident[:, :])
                ins.then_inc(wT_ready, 1)
                return ins

            def fold_products(n, b):
                pe.wait_ge(wT_hi_done, n + 1)
                pe.wait_ge(wT_lo_done, n + 1)
                if not (isinstance(n, int) and n < 2):
                    pe.wait_ge(fold_lo_done, n - 1)
                m = 0
                for c in range(KH):
                    for part, other in ((0, ow_hi), (0, ow_lo), (1, ow_hi)):
                        ins = nc.tensor.matmul(ps[:, 6 + b, 0:O], wT[:, b, part, c, :], other[:, c, :],
                                               start=m == 0, stop=m == 3 * KH - 1)
                        m += 1
                ins.then_inc(fold_ready, 1)

            pe.wait_ge(small_ready, 3)
            pe.wait_ge(ew_loaded[0], 16)
            weight_transposes(0, 0, 0, 0)
            pe.wait_ge(ebT_lo_done, 1)
            m = 0
            for c in range(KH):
                for part, other in ((ebT_hi, ow_hi), (ebT_hi, ow_lo), (ebT_lo, ow_hi)):
                    ins = nc.tensor.matmul(ps[0:64, 7, 0:O], part[:, c, :], other[:, c, :],
                                           start=m == 0, stop=m == 3 * KH - 1)
                    m += 1
            ins.then_inc(bias_acc, 1)
            weight_transposes(1, 1, 0, 1)
            fold_products(0, 0)
            for e in range(1, NE):
                pe.wait_ge(ew_loaded[e % WS], 16 * (e // WS + 1))
                weight_transposes(2 * e, 0, e % WS, 0)
                if e == 1:
                    pe.wait_ge(bias_step, 1)
                fold_products(2 * e - 1, 1)
                weight_transposes(2 * e + 1, 1, e % WS, 1)
                fold_products(2 * e, 0)
            fold_products(2 * NE - 1, 1)

            def attend(i, b):
                if not (isinstance(i, int) and i < 2):
                    pe.wait_ge(x1_done, i - 1)
                m = 0
                for j in range(NS):
                    r = P if j < NF else REST
                    for left, right in ((p_hi, ctxn_hi), (p_hi, ctxn_lo), (p_lo, ctxn_hi)):
                        ins = nc.tensor.matmul(ps[:, C_BANK + b, 0:D], left[0:r, j, bass.ds(i * P, P)], right[0:r, j, :],
                                               start=m == 0, stop=m == 3 * NS - 1)
                        m += 1
                ins.then_inc(c_ready, 1)

            def y2_transposes(i, b):
                pe.wait_ge(y2_ready, i + 1)
                if not (isinstance(i, int) and i < 1):
                    pe.wait_ge(y2T_lo_done, i)
                for k in range(KD):
                    ins = nc.tensor.transpose(ps[:, T_BANK, k * P:(k + 1) * P], y2[:, b, k * P:(k + 1) * P], ident[:, :])
                ins.then_inc(y2T_ready, 1)

            def logits(i, b):
                pe.wait_ge(y2T_hi_done, i + 1)
                pe.wait_ge(y2T_lo_done, i + 1)
                if not (isinstance(i, int) and i < 1):
                    pe.wait_ge(acc_done, (NE + 1) * (i - 1) + 1)
                m = 0
                for k in range(KD):
                    for part, other in ((0, gw_hi), (0, gw_lo), (1, gw_hi)):
                        ins = nc.tensor.matmul(logits_ps, y2T[:, b, part, k, :], other[:, k, :], start=m == 0, stop=m == 3 * KD - 1)
                        m += 1
                ins.then_inc(logits_ready, 1)

            def onehot_transpose(i):
                pe.wait_ge(onehot_ready, i + 1)
                nc.tensor.transpose(ps16[:, 0:P], onehot[:, :], ident16[:, :]).then_inc(onehotT_ready, 1)

            def bias_product(i):
                pe.wait_ge(onehotT_done, i + 1)
                nc.tensor.matmul(bias_ps, onehotT[0:64, :], bias2[:, :], start=True, stop=True).then_inc(bias_ready, 1)

            def experts(i, b):
                for q in range(NB):
                    if not (isinstance(i, int) and i < 1):
                        pe.wait_ge(acc_done, (NE + 1) * (i - 1) + EPB * (q + 1) + 1)
                    m = 0
                    for k in range(KD):
                        for part, other in ((0, fold_hi), (0, fold_lo), (1, fold_hi)):
                            ins = nc.tensor.matmul(ps[:, FFN_BANK + q, :], y2T[:, b, part, k, :], other[:, k, q * BANK:(q + 1) * BANK],
                                                   start=m == 0, stop=m == 3 * KD - 1)
                            m += 1
                    ins.then_inc(bank_ready, 1)
                    if q == 0:
                        bias_product(i)

            pe.wait_ge(exp_done, NS)
            pe.wait_ge(p_lo_ready, NS)
            pe.wait_ge(p_hi_ready, NS)
            pe.wait_ge(ctxn_ready, NS)
            attend(0, 0)
            pe.wait_ge(fold_hi_done, 2 * NE)
            pe.wait_ge(fold_lo_done, 2 * NE)
            pe.wait_ge(bias_step, 5)
            attend(1, 1)
            y2_transposes(0, 0)
            logits(0, 0)

            def steps(s):
                for u in range(2):
                    attend(s + u, u)
                    onehot_transpose(s + u - 2)
                    y2_transposes(s + u - 1, 1 - u)
                    experts(s + u - 2, u)
                    logits(s + u - 1, 1 - u)

            steps(2)
            with pe.Fori(2, NT // 2) as h:
                steps(2 * h)
            onehot_transpose(NT - 2)
            y2_transposes(NT - 1, 1)
            experts(NT - 2, 0)
            logits(NT - 1, 1)
            onehot_transpose(NT - 1)
            experts(NT - 1, 1)


_INS = ['x', 'ctx_1024', 'g_xattn', 'g_ffn', 'L0_ffn_gate_w', 'L0_ffn_gate_b', 'L0_ffn_expert_w', 'L0_ffn_expert_b',
        'L0_ffn_out_w', 'L0_ffn_out_b']
_OUTS = [((1, 2048, 256), 'float32')]


def kernel(**inputs):
    import numpy as _np
    import concourse.bacc as _bacc
    from concourse import mybir as _mybir
    from concourse.bass_utils import run_bass_kernel_spmd as _run

    nc = _bacc.Bacc("TRN2", target_bir_lowering=False, num_devices=1)
    arrays, args = {}, []
    for name in _INS:
        a = _np.ascontiguousarray(inputs[name])
        arrays[f"in_{name}_dram"] = a
        args.append(nc.dram_tensor(f"in_{name}_dram", a.shape, _mybir.dt.from_np(a.dtype), kind="ExternalInput").ap())
    for i, (shape, dtype) in enumerate(_OUTS):
        dt = _mybir.dt.from_np(_np.dtype(dtype))
        args.append(nc.dram_tensor(f"out_{i}_dram", shape, dt, kind="ExternalOutput").ap())
    bass_flamingo_gated_block(nc, *args)
    r = _run(nc, [arrays], core_ids=[0])
    got = tuple(r.results[0][f"out_{i}_dram"] for i in range(len(_OUTS)))
    return got[0]
```

```python
from contextlib import ExitStack

import concourse.bass as bass
from concourse import mybir

ALU = mybir.AluOpType
ACT = mybir.ActivationFunctionType
F32 = mybir.dt.float32
F16 = mybir.dt.float16
I32 = mybir.dt.int32
AX_X = mybir.AxisListType.X

P = 128
BANK = 512

LN2 = 0.6931471805599453
PROB_SHIFT = 10 * LN2
CTX_SCALE = 2.0 ** 16
C_UNSCALE = 2.0 ** -16
W_SCALE = 2.0 ** 8
M_SCALE = 2.0 ** -8
OUT_UNSCALE = 2.0 ** -8
EPS = 1e-5


def bass_flamingo_gated_block(
    nc: bass.Bass,
    x: bass.AP,
    ctx_rows: bass.AP,
    ctx_cols: bass.AP,
    g_xattn: bass.AP,
    g_ffn: bass.AP,
    gate_w: bass.AP,
    gate_b: bass.AP,
    expert_wt: bass.AP,
    expert_bt: bass.AP,
    out_w: bass.AP,
    out_b: bass.AP,
    out: bass.AP,
):
    _, T, D = x.shape
    S = ctx_rows.shape[1]
    NE, H, _ = expert_wt.shape
    O = out_w.shape[1]
    NT = T // P
    NS = -(-S // P)
    NF = S // P
    REST = S - NF * P
    KD = D // P
    KH = H // P
    NC = T // BANK
    WS = 3
    WU = 8
    NU = NE * KD
    XG = 4
    NX = NT // XG
    POOL_T = T - BANK
    NSL = NT + NE - 1
    ROW = D + 3
    R_RS, R_NMR, R_ID = D, D + 1, D + 2
    NOBODY = 1 << 20
    REGION = T + P
    EMPTY0 = NE * REGION
    assert KD == 2 and NC == 4 and NS == NF + 1 and NF % 2 == 0 and D == O == 256

    def below(i, n):
        return isinstance(i, int) and i < n

    with ExitStack() as stack:
        def sb(name, shape, dt):
            return stack.enter_context(nc.sbuf_tensor(name, shape, dt))

        def sem(name):
            return stack.enter_context(nc.semaphore(name))

        xr = sb("xr", [P, NT, ROW], F32)
        xt = xr[:, :, 0:D]
        xr_id = xr[:, :, :].bitcast(I32)[:, :, R_ID]
        ctx = sb("ctx", [P, NS, D], F32)
        prob = sb("prob", [P, 2, T], F32)
        ynorm = prob[:, :, :].rearrange("p b (t d) -> p (b t) d", d=D)
        wT = prob[:, :, :].rearrange("p b t -> p (b t)").bitcast(F16).rearrange(
            "p (u s c d) -> p u s c d", u=WU, s=2, c=KH)
        yT_hi = sb("yT_hi", [P, KD, T], F16)
        yT_lo = sb("yT_lo", [P, KD, T], F16)
        fold_hi, fold_lo = yT_hi, yT_lo
        cT_hi = sb("cT_hi", [P, NS, D], F16)
        cT_lo = sb("cT_lo", [P, NS, D], F16)
        ctxn_hi, ctxn_lo = cT_hi, cT_lo
        p_hi = sb("p_hi", [P, NS, T], F16)
        p_lo = sb("p_lo", [P, NS, T], F16)
        ow = p_lo[:, NF, :].bitcast(F32).rearrange("p (c o) -> p c o", c=KH)
        srt = p_lo[:, :, :].rearrange("p j t -> p (j t)")[:, 0:NSL * ROW * 2].bitcast(F32).rearrange("p (s w) -> p s w", w=ROW)
        srt_id = p_lo[:, :, :].rearrange("p j t -> p (j t)")[:, 0:NSL * ROW * 2].bitcast(I32).rearrange("p (s w) -> p s w", w=ROW)
        bias2 = p_hi[0:2, 0, 0:NE * O]
        stage = sb("stage", [P, KD * S], F32)
        ctxT = stage[:, :].rearrange("p (k s) -> p k s", k=KD)
        ew = stage[:, 0:WS * KH * D].rearrange("p (w c d) -> p w c d", w=WS, c=KH)
        late = ctx[:, :, :].rearrange("p j d -> p (j d)")
        y2 = late[:, 0:4 * D].rearrange("p (b d) -> p b d", b=4)
        y2T = late[:, 4 * D:8 * D].bitcast(F16).rearrange("p (b s k t) -> p b s k t", b=4, s=2, k=KD)
        bias_f = late[0:NE, 8 * D:9 * D]
        bias_hl = late[0:NE, 9 * D:10 * D].bitcast(F16).rearrange("e (s o) -> e s o", s=2)
        rest = 10 * D
        full = late[:, rest:rest + NE * NT].rearrange("p (e n) -> p e n", e=NE)
        before = late[:, rest + NE * NT:rest + NE * (NT + NE)].rearrange("p (e f) -> p e f", e=NE)
        rest += NE * (NT + NE)
        ended, begun, where = [late[:, rest + n * NSL * NE:rest + (n + 1) * NSL * NE].rearrange("p (s e) -> p s e", e=NE)
                               for n in range(3)]
        empty = sb("empty", [P, ROW], F32)
        empty_id = empty[:, :].bitcast(I32)[:, R_ID:R_ID + 1]
        ow_hi = sb("ow_hi", [P, KH, O], F16)
        ow_lo = sb("ow_lo", [P, KH, O], F16)
        eb = sb("eb", [P, KH, NE], F32)
        eb_hi = sb("eb_hi", [P, KH, NE], F16)
        eb_lo = sb("eb_lo", [P, KH, NE], F16)
        ob = sb("ob", [NE, O], F32)
        gw = sb("gw", [P, KD, NE], F32)
        gw_hi = sb("gw_hi", [P, KD, NE], F16)
        gw_lo = sb("gw_lo", [P, KD, NE], F16)
        gb = sb("gb", [P, NE], F32)
        gates = sb("gates", [P, 2], F32)
        tgates = sb("tgates", [P, 2], F32)
        gscale = sb("gscale", [P, 3], F32)
        ctxn = sb("ctxn", [P, D], F32)
        ident = sb("ident", [P, P], F32)
        ones16 = sb("ones16", [P, P], F16)
        lower16 = sb("lower16", [P, P], F16)
        desc = sb("desc", [P, NE], F32)
        count_i = sb("count_i", [P, NSL], I32)
        first_i = sb("first_i", [P, NE], I32)
        where_i = sb("where_i", [P, NSL, NE], I32)
        first = sb("first", [P, NE], F32)
        where0 = sb("where0", [P, NSL, NE], F32)
        slots = sb("slots", [P, NSL], F32)
        thr = sb("thr", [P, NT], F32)
        earlier = sb("earlier", [P, NE, NE], F32)
        eps = sb("eps", [P, 1], F32)
        held = sb("held", [P, 1], F32)
        stat6 = sb("stat6", [P, NT, 6], F32)
        stat2 = sb("stat2", [P, NT, 2], F32)
        sd = sb("sd", [P, NT], F32)
        rs = sb("rs", [P, NT], F32)
        newt = sb("newt", [P, NT], F32)
        nmr = sb("nmr", [P, NT], F32)
        smax = sb("smax", [P, NS], F32)
        nbias = sb("nbias", [P, NS], F32)
        zsum = sb("zsum", [P, NS], F32)
        rz = sb("rz", [P, NS], F32)
        bstat6 = sb("bstat6", [P, 2, 6], F32)
        bstat2 = sb("bstat2", [P, 2, 2], F32)
        bsd = sb("bsd", [P, 2], F32)
        lg = sb("lg", [P, NE], F32)
        lmax = sb("lmax", [P, 1], F32)
        wsel = sb("wsel", [P, NE], F32)
        wmax = sb("wmax", [P, 1], F32)
        onehot = sb("onehot", [P, NT, NE], F16)
        seen = sb("seen", [P, NT + 1, NE], F16)
        placing = sb("placing", [P, NE], F32)
        place = sb("place", [P, NT], I32)
        tiles = sb("tiles", [P, NE], F32)
        start = sb("start", [P, NE], F32)
        end = sb("end", [P, NE], F32)
        slot_f = sb("slot_f", [P, NSL], F32)
        slot_off = sb("slot_off", [P, NSL], I32)
        slot_row = sb("slot_row", [P, NSL], I32)
        pad_row = sb("pad_row", [P, NE], I32)

        ps = stack.enter_context(nc.psum_tensor("ps", [P, 8, BANK], F32))
        C_BANKS, FOLD_BANKS, T_BANKS, G_BANK, R_BANK = (7, 5), (2, 3), (6, 0), 1, 4
        logits_ps = ps[:, G_BANK, 0:NE]
        rank_ps = ps[:, R_BANK, 0:NE]
        count_ps = ps[:, R_BANK, NE:2 * NE]
        sorted_rows = nc.dram_tensor("sorted_rows", [NE * REGION + P, ROW], F32, kind="Internal").ap()

        def sems(text):
            return [sem(name) for name in text.split()]

        x_loaded = [sem(f"x_loaded{g}") for g in range(NX)]
        ctxT_loaded = [sem(f"ctxT_loaded{g}") for g in range(3)]
        ew_loaded = [sem(f"ew_loaded{w}") for w in range(WS)]
        slot_loaded = [sem(f"slot_loaded{s}") for s in range(NSL)]
        ctx_loaded, small_loaded, ow_loaded, bias_loaded, bias_spread = sems(
            "ctx_loaded small_loaded ow_loaded bias_loaded bias_spread")
        emptied, sorted_out, padded, out_stored = sems("emptied sorted_out padded out_stored")
        ident_zeroed, eps_ready, ident_ready, consts_ready, empty_ready, iota_done = sems(
            "ident_zeroed eps_ready ident_ready consts_ready empty_ready iota_done")
        stat6_done, stat2_done, sd_ready, rs_done, nmr_done, y_act, y_dve, y_pool = sems(
            "stat6_done stat2_done sd_ready rs_done nmr_done y_act y_dve y_pool")
        tr_ready, tr_hi_done, tr_lo_done, cT_hi_done, cT_ready = sems(
            "tr_ready tr_hi_done tr_lo_done cT_hi_done cT_ready")
        tanh_done, gscale_ready, w_hi_done, w_ready = sems("tanh_done gscale_ready w_hi_done w_ready")
        scores_ready, smax_done, nbias_ready, exp_done, p_hi_ready, p_lo_ready, p_lo_pool_ready = sems(
            "scores_ready smax_done nbias_ready exp_done p_hi_ready p_lo_ready p_lo_pool_ready")
        rz_ready, ctxn_done, ctxn_hi_done, ctxn_ready = sems("rz_ready ctxn_done ctxn_hi_done ctxn_ready")
        bias_acc, bias_step = sems("bias_acc bias_step")
        wT_hi_done, wT_lo_done, fold_ready, fold_hi_done, fold_lo_done = sems(
            "wT_hi_done wT_lo_done fold_ready fold_hi_done fold_lo_done")
        c_ready, x1_done, b6_done, b2_done, bsd_ready, brs_done, bnmr_ready = sems(
            "c_ready x1_done b6_done b2_done bsd_ready brs_done bnmr_ready")
        y2_ready, y2T_ready, y2T_hi_done, y2T_lo_done = sems("y2_ready y2T_ready y2T_hi_done y2T_lo_done")
        logits_ready, lg_done, lmax_done, wsel_done, wmax_done, onehot_ready, seen_ready = sems(
            "logits_ready lg_done lmax_done wsel_done wmax_done onehot_ready seen_ready")
        rank_ready, place_added, place_masked, place_ready = sems("rank_ready place_added place_masked place_ready")
        counts_ready, route_step, pad_row_ready, slot_off_ready, slot_row_ready = sems(
            "counts_ready route_step pad_row_ready slot_off_ready slot_row_ready")
        z_act, z_dve, zT_ready, zT_hi_done, zT_lo_done, o_ready, o_done = sems(
            "z_act z_dve zT_ready zT_hi_done zT_lo_done o_ready o_done")

        x_view = x.rearrange("a (p i) d -> p (a i) d", i=NT)
        out_rows = out.rearrange("a t d -> (a t) d")
        ctx_full = ctx_rows[:, 0:NF * P, :].rearrange("a (j p) d -> p (a j) d", p=P)
        ctx_rest = ctx_rows[0, NF * P:S, :]
        ctxT_view = ctx_cols.rearrange("(k p) s -> p k s", p=P)
        CT_CUTS = (0, 2 * P, 8 * P, S)

        def group_io(n):
            src = ps[:, 6 + n % 2, :].rearrange("p (k c) -> p k c", k=KD)
            return src, [t[:, :, 2 * n * P:2 * (n + 1) * P] for t in (yT_hi, yT_lo)]

        NG = NT // 2

        block = stack.enter_context(nc.Block())

        @block.sync
        def _(sp):
            sp.dma_start(xt[:, 0:XG, :], x_view[:, 0:XG, :]).then_inc(x_loaded[0], 16)
            for g in range(1, NX):
                sp.dma_start(xt[:, XG * g:XG * (g + 1), :], x_view[:, XG * g:XG * (g + 1), :]).then_inc(x_loaded[g], 16)
            for g in range(1, 3):
                a, b = CT_CUTS[g:g + 2]
                sp.dma_start(ctxT[:, :, a:b], ctxT_view[:, :, a:b]).then_inc(ctxT_loaded[g], 16)
            sp.dma_start(ow, out_w.rearrange("(c p) o -> p c o", p=P)).then_inc(ow_loaded, 16)
            sp.dma_start(ctx[:, 0:NF, :], ctx_full).then_inc(ctx_loaded, 16)
            sp.dma_start(ctx[0:REST, NF, :], ctx_rest).then_inc(ctx_loaded, 16)
            sp.dma_start(ob[:, :], out_b.rearrange("(a o) -> a o", a=1).broadcast_to([NE, O])).then_inc(bias_loaded, 16)
            sp.wait_ge(empty_ready, 2)
            sp.dma_start(sorted_rows[EMPTY0:EMPTY0 + P, :], empty[:, :]).then_inc(emptied, 16)
            sp.wait_ge(cT_ready, NS)
            for e in range(NE):
                if e >= WS:
                    sp.wait_ge(wT_lo_done, KD * (e - WS + 1))
                sp.dma_start(ew[:, e % WS, :, :], expert_wt[e].rearrange("(c p) d -> p c d", p=P)).then_inc(ew_loaded[e % WS], 16)
            sp.wait_ge(bias_step, 4)
            sp.wait_ge(c_ready, NT)
            for h in range(2):
                sp.dma_start(bias2[h:h + 1, :].rearrange("a (e o) -> a e o", e=NE),
                             bias_hl[:, h, :]).then_inc(bias_spread, 16)
            sp.wait_ge(pad_row_ready, 1)
            sp.wait_ge(sorted_out, 16 * NT)
            for e in range(NE):
                row = nc.sync.value_load(pad_row[0:1, e:e + 1], min_val=e * REGION, max_val=e * REGION + T)
                sp.dma_start(sorted_rows[bass.ds(row, P), :], empty[:, :]).then_inc(padded, 16)
            sp.wait_ge(slot_row_ready, 1)
            sp.wait_ge(padded, 16 * NE)
            sp.wait_ge(emptied, 16)
            for s in range(NSL):
                row = nc.sync.value_load(slot_row[0:1, s:s + 1], min_val=0, max_val=EMPTY0)
                sp.dma_start(srt[:, s, :], sorted_rows[bass.ds(row, P), :]).then_inc(slot_loaded[s], 16)
            sp.wait_ge(out_stored, 16 * NSL)

        @block.gpsimd
        def _(pool):
            nc.gpsimd.memset(eps[:, :], EPS).then_inc(eps_ready, 1)
            nc.gpsimd.memset(ident[:, :], 0.0).then_inc(ident_zeroed, 1)
            pool.wait_ge(ident_zeroed, 1)
            nc.gpsimd.affine_select(out=ident[:, :], in_=ident[:, :], compare_op=ALU.not_equal, fill=1.0,
                                    base=0, pattern=[[-1, P]], channel_multiplier=1).then_inc(ident_ready, 1)

            def split_columns(j, r):
                hi, lo = [t[:, j, :].rearrange("p (k c) -> p k c", k=KD)[:, :, 0:r] for t in (cT_hi, cT_lo)]
                src = ctxT[:, :, j * P:j * P + r]
                nc.gpsimd.tensor_copy(hi, src).then_inc(cT_hi_done, 1)
                pool.wait_ge(cT_hi_done, j + 1)
                nc.gpsimd.tensor_tensor(lo, src, hi, ALU.subtract).then_inc(cT_ready, 1)

            def norm_tile(g):
                i = XG * g + 3
                pool.wait_ge(nmr_done, g + 1)
                nc.gpsimd.tensor_scalar(ynorm[:, i, :], xt[:, i, :], rs[:, i:i + 1], nmr[:, i:i + 1],
                                        ALU.mult, ALU.add).then_inc(y_pool, 1)

            pool.wait_ge(ctxT_loaded[0], 16)
            split_columns(0, P)
            norm_tile(0)
            split_columns(1, P)
            pool.wait_ge(ctxT_loaded[1], 16)
            for g in range(1, NX):
                norm_tile(g)
                split_columns(g + 1, P)
            for j in range(NX + 1, 8):
                split_columns(j, P)
            pool.wait_ge(ctxT_loaded[2], 16)
            for j in range(8, NS):
                split_columns(j, P if j < NF else REST)
            nc.gpsimd.memset(empty[:, :], 0.0).then_inc(empty_ready, 1)
            pool.wait_ge(empty_ready, 1)
            nc.gpsimd.memset(empty_id, NOBODY).then_inc(empty_ready, 1)
            nc.gpsimd.memset(ones16[:, :], 1.0).then_inc(iota_done, 1)
            nc.gpsimd.memset(lower16[:, :], 1.0).then_inc(iota_done, 1)
            nc.gpsimd.memset(earlier[:, :, :], 1.0).then_inc(iota_done, 1)
            nc.gpsimd.iota(count_i[:, :], pattern=[[1, NSL]], base=0, channel_multiplier=0).then_inc(iota_done, 1)
            nc.gpsimd.iota(first_i[:, :], pattern=[[REGION, NE]], base=0, channel_multiplier=0).then_inc(iota_done, 1)
            nc.gpsimd.iota(where_i[:, :, :], pattern=[[P, NSL], [REGION, NE]], base=-EMPTY0, channel_multiplier=0).then_inc(iota_done, 1)
            pool.wait_ge(iota_done, 6)
            nc.gpsimd.affine_select(out=lower16[:, :], in_=lower16[:, :], compare_op=ALU.is_gt, fill=0.0,
                                    base=0, pattern=[[1, P]], channel_multiplier=-1).then_inc(consts_ready, 1)
            nc.gpsimd.affine_select(out=earlier[:, :, :], in_=earlier[:, :, :], compare_op=ALU.is_gt, fill=0.0,
                                    base=0, pattern=[[1, NE], [-1, NE]], channel_multiplier=0).then_inc(consts_ready, 1)
            nc.gpsimd.tensor_copy(slots[:, :], count_i[:, :]).then_inc(consts_ready, 1)
            nc.gpsimd.tensor_scalar(thr[:, :], count_i[:, 0:NT], float(P), None, ALU.mult).then_inc(consts_ready, 1)
            nc.gpsimd.tensor_copy(first[:, :], first_i[:, :]).then_inc(consts_ready, 1)
            nc.gpsimd.tensor_copy(where0[:, :, :], where_i[:, :, :]).then_inc(consts_ready, 1)
            nc.gpsimd.memset(seen[:, 0, :], 0.0).then_inc(consts_ready, 1)
            for e in range(NE):
                nc.gpsimd.memset(desc[:, e:e + 1], float(NE - e)).then_inc(consts_ready, 1)
            nc.gpsimd.iota(xr_id, pattern=[[1, NT]], base=0, channel_multiplier=NT).then_inc(consts_ready, 1)

            def normalise_context(j, b, r):
                hi = ctxn_hi[0:r, bass.ds(j, 1), :].rearrange("p a d -> p (a d)")
                lo = ctxn_lo[0:r, bass.ds(j, 1), :].rearrange("p a d -> p (a d)")
                pool.wait_ge(ctxn_done, j + 1)
                nc.gpsimd.tensor_copy(hi, ctxn[0:r, :]).then_inc(ctxn_hi_done, 1)
                pool.wait_ge(ctxn_hi_done, j + 1)
                nc.gpsimd.tensor_tensor(lo, ctxn[0:r, :], hi, ALU.subtract).then_inc(ctxn_ready, 1)
                pool.wait_ge(p_hi_ready, j + 1)
                nc.gpsimd.tensor_tensor(p_lo[0:r, bass.ds(j, 1), POOL_T:T].rearrange("p a t -> p (a t)"), prob[0:r, b, POOL_T:T],
                                        p_hi[0:r, bass.ds(j, 1), POOL_T:T].rearrange("p a t -> p (a t)"),
                                        ALU.subtract).then_inc(p_lo_pool_ready, 1)

            with pool.Fori(0, NF // 2) as h:
                normalise_context(2 * h, 0, P)
                normalise_context(2 * h + 1, 1, P)
            normalise_context(NF, 0, REST)

            for i in range(NT):
                pool.wait_ge(place_ready, i + 1)
                pool.wait_ge(bnmr_ready, i + 1)
                nc.gpsimd.indirect_dma_start(sorted_rows, bass.IndirectOffsetOnAxis(ap=place[:, i:i + 1], axis=0),
                                             xr[:, i, :], None).then_inc(sorted_out, 16)
            for s in range(NSL):
                pool.wait_ge(o_done, s + 1)
                nc.gpsimd.indirect_dma_start(out_rows, bass.IndirectOffsetOnAxis(ap=srt_id[:, s, R_ID:R_ID + 1], axis=0),
                                             srt[:, s, 0:D], None, bounds_check=T - 1, oob_is_err=False).then_inc(out_stored, 16)

        @block.scalar
        def _(act):
            act.dma_start(ctxT[:, :, 0:CT_CUTS[1]], ctxT_view[:, :, 0:CT_CUTS[1]]).then_inc(ctxT_loaded[0], 16)
            act.dma_start(gates[:, 0:1], g_xattn.rearrange("(a b) -> a b", a=1).broadcast_to([P, 1])).then_inc(small_loaded, 16)
            act.dma_start(gates[:, 1:2], g_ffn.rearrange("(a b) -> a b", a=1).broadcast_to([P, 1])).then_inc(small_loaded, 16)
            act.dma_start(gw[:, :, :], gate_w.rearrange("(k p) e -> p k e", p=P)).then_inc(small_loaded, 16)
            act.dma_start(gb[:, :], gate_b.rearrange("(a e) -> a e", a=1).broadcast_to([P, NE])).then_inc(small_loaded, 16)
            act.dma_start(eb[:, :, :], expert_bt.rearrange("(c p) e -> p c e", p=P)).then_inc(small_loaded, 16)
            act.wait_ge(eps_ready, 1)
            nc.scalar.activation(bsd[:, 0:1], eps[:, 0:1], ACT.Sqrt)

            def root(g):
                act.wait_ge(stat2_done, XG * (g + 1))
                nc.scalar.activation(sd[:, XG * g:XG * (g + 1)], stat2[:, XG * g:XG * (g + 1), 1], ACT.Sqrt,
                                     bias=eps[:, 0:1]).then_inc(sd_ready, 1)

            def norm_tiles(g):
                act.wait_ge(nmr_done, g + 1)
                for i in range(XG * g, XG * g + 2):
                    nc.scalar.activation(ynorm[:, i, :], xt[:, i, :], ACT.Identity, bias=nmr[:, i:i + 1],
                                         scale=rs[:, i:i + 1]).then_inc(y_act, 1)

            def group_high(n):
                src, (hi, _) = group_io(n)
                act.wait_ge(tr_ready, n + 1)
                nc.scalar.activation(hi, src, ACT.Copy).then_inc(tr_hi_done, 1)

            root(0)
            for g in range(NX):
                norm_tiles(g)
                if g + 1 < NX:
                    root(g + 1)
                if g:
                    group_high(2 * g - 2)
                    group_high(2 * g - 1)
            group_high(NG - 2)
            group_high(NG - 1)
            act.wait_ge(small_loaded, 80)
            nc.scalar.activation(tgates[:, :], gates[:, :], ACT.Tanh).then_inc(tanh_done, 1)

            def softmax(j, b, r):
                act.wait_ge(nbias_ready, j + 1)
                if not below(j, 2):
                    act.wait_ge(p_lo_ready, j - 1)
                    act.wait_ge(p_lo_pool_ready, j - 1)
                nc.scalar.activation(prob[0:r, b, :], ps[0:r, 4 * b:4 * b + 4, :].rearrange("p a c -> p (a c)"), ACT.Exp,
                                     bias=nbias[0:r, bass.ds(j, 1)], accum_out=zsum[0:r, bass.ds(j, 1)]).then_inc(exp_done, 1)
                act.wait_ge(exp_done, j + 1)
                nc.scalar.activation(p_hi[0:r, bass.ds(j, 1), :].rearrange("p a t -> p (a t)"), prob[0:r, b, :],
                                     ACT.Copy).then_inc(p_hi_ready, 1)

            softmax(0, 0, P)
            softmax(1, 1, P)
            act.wait_ge(ow_loaded, 16)
            nc.scalar.activation(ow_hi[:, :, :], ow, ACT.Copy, scale=W_SCALE).then_inc(w_hi_done, 1)
            nc.scalar.activation(eb_hi[:, :, :], eb[:, :, :], ACT.Copy, scale=W_SCALE).then_inc(w_hi_done, 1)
            nc.scalar.activation(gw_hi[:, :, :], gw[:, :, :], ACT.Copy, scale=W_SCALE).then_inc(w_hi_done, 1)
            with act.Fori(1, NF // 2) as h:
                softmax(2 * h, 0, P)
                softmax(2 * h + 1, 1, P)
            act.wait_ge(w_ready, 3)
            softmax(NF, 0, REST)

            def weight_hi(n):
                e, k = n // KD, n % KD
                act.wait_ge(ew_loaded[e % WS], 16 * (e // WS + 1))
                if n >= WU:
                    act.wait_ge(fold_ready, n - WU + 1)
                nc.scalar.activation(wT[:, n % WU, 0, :, :], ew[:, e % WS, :, k * P:(k + 1) * P], ACT.Copy,
                                     scale=W_SCALE).then_inc(wT_hi_done, 1)

            def fold_hi_copy(n):
                e, k = n // KD, n % KD
                act.wait_ge(fold_ready, n + 1)
                nc.scalar.activation(fold_hi[:, k, e * O:(e + 1) * O], ps[:, FOLD_BANKS[n % 2], 0:O], ACT.Copy,
                                     scale=gscale[:, 1:2]).then_inc(fold_hi_done, 1)

            def y2T_out(i, b):
                act.wait_ge(y2T_ready, i + 1)
                if not below(i, 2):
                    act.wait_ge(logits_ready, i - 1)
                nc.scalar.activation(y2T[:, b, 0, :, :], ps[:, T_BANKS[0], 0:D].rearrange("p (k t) -> p k t", k=KD),
                                     ACT.Copy).then_inc(y2T_hi_done, 1)

            def norm2(i, b):
                act.wait_ge(b2_done, i + 1)
                nc.scalar.activation(bsd[:, b:b + 1], bstat2[:, b, 1:2], ACT.Sqrt, bias=eps[:, 0:1]).then_inc(bsd_ready, 1)
                act.wait_ge(bnmr_ready, i + 1)
                if not below(i, 2):
                    act.wait_ge(y2T_ready, i - 1)
                row = xr[:, bass.ds(i, 1), :].rearrange("p a d -> p (a d)")
                nc.scalar.activation(y2[:, b, :], row[:, 0:D], ACT.Identity, bias=row[:, R_NMR:R_NMR + 1],
                                     scale=row[:, R_RS:R_RS + 1]).then_inc(y2_ready, 1)

            act.wait_ge(ctxn_done, NS)
            act.wait_ge(p_lo_ready, NS)
            act.wait_ge(p_lo_pool_ready, NS)
            def step(s, u):
                y2T_out(s - 1, 1 - u)
                norm2(s, u)

            norm2(0, 0)
            for s in (1, 2, 3):
                for n in range((s - 1) * 3, min(s * 3, WU)):
                    weight_hi(n)
                step(s, s % 2)
            with act.Fori(2, NT // 2) as h:
                step(2 * h, 0)
                step(2 * h + 1, 1)
            fold_hi_copy(0)
            y2T_out(NT - 1, 1)
            for n in range(1, NU):
                if n + WU - 1 < NU:
                    weight_hi(n + WU - 1)
                fold_hi_copy(n)

            def slot_norm(s):
                act.wait_ge(slot_loaded[s], 16)
                if s >= 4:
                    act.wait_ge(zT_ready, s - 3)
                nc.scalar.activation(y2[:, s % 4, :], srt[:, s, 0:D], ACT.Identity, bias=srt[:, s, R_NMR:R_NMR + 1],
                                     scale=srt[:, s, R_RS:R_RS + 1]).then_inc(z_act, 1)

            def slot_hi(s):
                act.wait_ge(zT_ready, s + 1)
                if s >= 4:
                    act.wait_ge(o_ready, s - 3)
                nc.scalar.activation(y2T[:, s % 4, 0, :, :], ps[:, T_BANKS[s % 2], 0:D].rearrange("p (k t) -> p k t", k=KD),
                                     ACT.Copy).then_inc(zT_hi_done, 1)

            slot_norm(0)
            slot_norm(2)
            for s in range(NSL):
                slot_hi(s)
                if s % 2 == 0 and s + 4 < NSL:
                    slot_norm(s + 4)

        @block.vector
        def _(dve):
            def aggregate(g):
                dve.wait_ge(stat6_done, XG * (g + 1))
                for i in range(XG * g, XG * (g + 1)):
                    nc.vector.bn_aggr(stat2[:, i, :], stat6[:, i, :]).then_inc(stat2_done, 1)

            def scale(g):
                w = slice(XG * g, XG * (g + 1))
                m = 5 * g

                def statistic(h):
                    if g + 1 < NX:
                        i = XG * (g + 1) + h
                        nc.vector.bn_stats(stat6[:, i, :], xt[:, i, :]).then_inc(stat6_done, 1)

                dve.wait_ge(sd_ready, g + 1)
                nc.vector.reciprocal(rs[:, w], sd[:, w]).then_inc(rs_done, 1)
                if g + 1 < NX:
                    dve.wait_ge(x_loaded[g + 1], 16)
                statistic(0)
                dve.wait_ge(rs_done, m + 1)
                nc.vector.tensor_tensor(newt[:, w], rs[:, w], rs[:, w], ALU.mult).then_inc(rs_done, 1)
                statistic(1)
                dve.wait_ge(rs_done, m + 2)
                nc.vector.scalar_tensor_tensor(out=newt[:, w], in0=stat2[:, w, 1], scalar=EPS, in1=newt[:, w],
                                               op0=ALU.add, op1=ALU.mult).then_inc(rs_done, 1)
                statistic(2)
                dve.wait_ge(rs_done, m + 3)
                nc.vector.tensor_scalar(newt[:, w], newt[:, w], -0.5, 1.5, ALU.mult, ALU.add).then_inc(rs_done, 1)
                statistic(3)
                dve.wait_ge(rs_done, m + 4)
                nc.vector.tensor_tensor(rs[:, w], rs[:, w], newt[:, w], ALU.mult).then_inc(rs_done, 1)
                if g + 1 < NX:
                    aggregate(g + 1)
                dve.wait_ge(rs_done, m + 5)
                nc.vector.scalar_tensor_tensor(out=nmr[:, w], in0=stat2[:, w, 0], scalar=-1.0, in1=rs[:, w],
                                               op0=ALU.mult, op1=ALU.mult).then_inc(nmr_done, 1)

            def norm_tile(g):
                i = XG * g + 2
                dve.wait_ge(nmr_done, g + 1)
                nc.vector.tensor_scalar(ynorm[:, i, :], xt[:, i, :], rs[:, i:i + 1], nmr[:, i:i + 1],
                                        ALU.mult, ALU.add).then_inc(y_dve, 1)

            def group_low(n):
                src, (hi, lo) = group_io(n)
                dve.wait_ge(tr_hi_done, n + 1)
                nc.vector.tensor_tensor(lo, src, hi, ALU.subtract).then_inc(tr_lo_done, 1)

            dve.wait_ge(x_loaded[0], 16)
            for i in range(XG):
                nc.vector.bn_stats(stat6[:, i, :], xt[:, i, :]).then_inc(stat6_done, 1)
            aggregate(0)
            for g in range(NX):
                scale(g)
                norm_tile(g)
                if g:
                    group_low(2 * g - 2)
                    group_low(2 * g - 1)
            group_low(NG - 2)
            group_low(NG - 1)

            dve.wait_ge(tanh_done, 1)
            for n, (col, scale) in enumerate(((0, CTX_SCALE), (1, M_SCALE), (1, W_SCALE))):
                nc.vector.tensor_scalar(gscale[:, n:n + 1], tgates[:, col:col + 1], scale, None, ALU.mult).then_inc(gscale_ready, 1)

            def row_max(j, b, r):
                dve.wait_ge(scores_ready, j + 1)
                c = bass.ds(j, 1)
                nc.vector.tensor_reduce(smax[0:r, c], ps[0:r, 4 * b:4 * b + 4, :].rearrange("p a c -> p (a c)"), AX_X,
                                        ALU.max).then_inc(smax_done, 1)
                dve.wait_ge(smax_done, j + 1)
                nc.vector.tensor_scalar(nbias[0:r, c], smax[0:r, c], -1.0, PROB_SHIFT, ALU.mult, ALU.add).then_inc(nbias_ready, 1)

            def split_prob(j, b, r):
                c = bass.ds(j, 1)
                dve.wait_ge(exp_done, j + 1)
                nc.vector.reciprocal(rz[0:r, c], zsum[0:r, c]).then_inc(rz_ready, 1)
                dve.wait_ge(rz_ready, j + 1)
                if not below(j, 1):
                    dve.wait_ge(ctxn_ready, j)
                nc.vector.tensor_scalar(ctxn[0:r, :], ctx[0:r, c, :].rearrange("p a d -> p (a d)"), rz[0:r, c],
                                        gscale[0:r, 0:1], ALU.mult, ALU.mult).then_inc(ctxn_done, 1)
                dve.wait_ge(p_hi_ready, j + 1)
                nc.vector.tensor_tensor(p_lo[0:r, c, 0:POOL_T].rearrange("p a t -> p (a t)"), prob[0:r, b, 0:POOL_T],
                                        p_hi[0:r, c, 0:POOL_T].rearrange("p a t -> p (a t)"), ALU.subtract).then_inc(p_lo_ready, 1)

            row_max(0, 0, P)
            row_max(1, 1, P)
            dve.wait_ge(ctx_loaded, 32)
            split_prob(0, 0, P)
            for n, (part, whole, hi) in enumerate(((ow_lo[:, :, :], ow, ow_hi[:, :, :]), (eb_lo[:, :, :], eb[:, :, :], eb_hi[:, :, :]),
                                                   (gw_lo[:, :, :], gw[:, :, :], gw_hi[:, :, :]))):
                dve.wait_ge(w_hi_done, n + 1)
                nc.vector.scalar_tensor_tensor(out=part, in0=whole, scalar=W_SCALE, in1=hi, op0=ALU.mult,
                                               op1=ALU.subtract).then_inc(w_ready, 1)
            nc.vector.tensor_scalar(gb[:, :], gb[:, :], W_SCALE, None, ALU.mult).then_inc(w_ready, 1)
            with dve.Fori(1, NF // 2) as h:
                j = 2 * h
                row_max(j, 0, P)
                split_prob(j - 1, 1, P)
                row_max(j + 1, 1, P)
                split_prob(j, 0, P)
            row_max(NF, 0, REST)
            split_prob(NF - 1, 1, P)
            split_prob(NF, 0, REST)

            def weight_lo(n):
                e, k = n // KD, n % KD
                dve.wait_ge(wT_hi_done, n + 1)
                nc.vector.scalar_tensor_tensor(out=wT[:, n % WU, 1, :, :], in0=ew[:, e % WS, :, k * P:(k + 1) * P],
                                               scalar=W_SCALE, in1=wT[:, n % WU, 0, :, :], op0=ALU.mult,
                                               op1=ALU.subtract).then_inc(wT_lo_done, 1)

            def fold_lo_part(n):
                e, k = n // KD, n % KD
                dve.wait_ge(fold_hi_done, n + 1)
                w = slice(e * O, (e + 1) * O)
                nc.vector.scalar_tensor_tensor(out=fold_lo[:, k, w], in0=ps[:, FOLD_BANKS[n % 2], 0:O], scalar=gscale[:, 1:2],
                                               in1=fold_hi[:, k, w], op0=ALU.mult, op1=ALU.subtract).then_inc(fold_lo_done, 1)

            def folded_bias():
                dve.wait_ge(bias_acc, 1)
                dve.wait_ge(bias_loaded, 16)
                nc.vector.scalar_tensor_tensor(out=bias_f, in0=ps[0:NE, R_BANK, 0:O], scalar=C_UNSCALE, in1=ob[:, :],
                                               op0=ALU.mult, op1=ALU.add).then_inc(bias_step, 1)
                dve.wait_ge(bias_step, 1)
                nc.vector.tensor_scalar(bias_f, bias_f, gscale[0:NE, 2:3], None, ALU.mult).then_inc(bias_step, 1)
                dve.wait_ge(bias_step, 2)
                nc.vector.tensor_copy(bias_hl[:, 0, :], bias_f).then_inc(bias_step, 1)
                dve.wait_ge(bias_step, 3)
                nc.vector.tensor_tensor(bias_hl[:, 1, :], bias_f, bias_hl[:, 0, :], ALU.subtract).then_inc(bias_step, 1)

            def choose(i):
                last = not below(i, 1)
                dve.wait_ge(logits_ready, i + 1)
                nc.vector.tensor_tensor(lg[:, :], logits_ps, gb[:, :], ALU.add).then_inc(lg_done, 1)
                if last:
                    place_add(i - 1)
                dve.wait_ge(lg_done, i + 1)
                nc.vector.tensor_reduce(lmax[:, :], lg[:, :], AX_X, ALU.max).then_inc(lmax_done, 1)
                if last:
                    place_mask(i - 1)
                dve.wait_ge(lmax_done, i + 1)
                nc.vector.scalar_tensor_tensor(out=wsel[:, :], in0=lg[:, :], scalar=lmax[:, 0:1], in1=desc[:, :],
                                               op0=ALU.is_equal, op1=ALU.mult).then_inc(wsel_done, 1)
                if last:
                    place_sum(i - 1)
                dve.wait_ge(wsel_done, i + 1)
                nc.vector.tensor_reduce(wmax[:, :], wsel[:, :], AX_X, ALU.max).then_inc(wmax_done, 1)
                dve.wait_ge(wmax_done, i + 1)
                nc.vector.tensor_scalar(onehot[:, bass.ds(i, 1), :].rearrange("p a e -> p (a e)"), wsel[:, :], wmax[:, 0:1],
                                        None, ALU.is_equal).then_inc(onehot_ready, 1)
                dve.wait_ge(onehot_ready, i + 1)
                nc.vector.tensor_tensor(seen[:, bass.ds(i + 1, 1), :], seen[:, bass.ds(i, 1), :], onehot[:, bass.ds(i, 1), :],
                                        ALU.add).then_inc(seen_ready, 1)

            def place_add(i):
                dve.wait_ge(rank_ready, i + 1)
                nc.vector.tensor_tensor(placing[:, :], rank_ps, first[:, :], ALU.add).then_inc(place_added, 1)

            def place_mask(i):
                dve.wait_ge(place_added, i + 1)
                nc.vector.tensor_tensor(placing[:, :], placing[:, :], onehot[:, bass.ds(i, 1), :].rearrange("p a e -> p (a e)"),
                                        ALU.mult).then_inc(place_masked, 1)

            def place_sum(i):
                dve.wait_ge(place_masked, i + 1)
                with nc.allow_low_precision(reason="small whole numbers"):
                    nc.vector.tensor_reduce(place[:, bass.ds(i, 1)], placing[:, :], AX_X, ALU.add).then_inc(place_ready, 1)

            def residual(i, b):
                row = xr[:, bass.ds(i, 1), :].rearrange("p a d -> p (a d)")
                dve.wait_ge(c_ready, i + 1)
                nc.vector.scalar_tensor_tensor(out=row[:, 0:D], in0=ps[:, C_BANKS[b], 0:D], scalar=C_UNSCALE, in1=row[:, 0:D],
                                               op0=ALU.mult, op1=ALU.add).then_inc(x1_done, 1)
                dve.wait_ge(x1_done, i + 1)
                nc.vector.memset(held[:, :], 0.0)
                nc.vector.bn_stats(bstat6[:, b, :], row[:, 0:D]).then_inc(b6_done, 1)
                dve.wait_ge(b6_done, i + 1)
                nc.vector.memset(held[:, :], 0.0)
                nc.vector.bn_aggr(bstat2[:, b, :], bstat6[:, b, :]).then_inc(b2_done, 1)

            def residual_scale(i, b):
                row = xr[:, bass.ds(i, 1), :].rearrange("p a d -> p (a d)")
                dve.wait_ge(bsd_ready, i + 1)
                nc.vector.reciprocal(row[:, R_RS:R_RS + 1], bsd[:, b:b + 1]).then_inc(brs_done, 1)
                dve.wait_ge(brs_done, i + 1)
                nc.vector.scalar_tensor_tensor(out=row[:, R_NMR:R_NMR + 1], in0=bstat2[:, b, 0:1], scalar=-1.0,
                                               in1=row[:, R_RS:R_RS + 1], op0=ALU.mult, op1=ALU.mult).then_inc(bnmr_ready, 1)

            def y2T_low(i, b):
                dve.wait_ge(y2T_hi_done, i + 1)
                nc.vector.tensor_tensor(y2T[:, b, 1, :, :], ps[:, T_BANKS[0], 0:D].rearrange("p (k t) -> p k t", k=KD),
                                        y2T[:, b, 0, :, :], ALU.subtract).then_inc(y2T_lo_done, 1)

            def route():
                step = [0]

                def done(ins):
                    step[0] += 1
                    ins.then_inc(route_step, 1)
                    dve.wait_ge(route_step, step[0])

                dve.wait_ge(counts_ready, 1)
                nc.vector.tensor_tensor(pad_row[:, :], count_ps, first[:, :], ALU.add).then_inc(pad_row_ready, 1)
                done(nc.vector.tensor_tensor(full, count_ps.unsqueeze(2).broadcast_to([P, NE, NT]),
                                             thr[:, :].unsqueeze(1).broadcast_to([P, NE, NT]), ALU.is_gt))
                done(nc.vector.tensor_reduce(tiles[:, :], full, AX_X, ALU.add))
                done(nc.vector.tensor_tensor(before, tiles[:, :].unsqueeze(1).broadcast_to([P, NE, NE]), earlier[:, :, :], ALU.mult))
                done(nc.vector.tensor_reduce(start[:, :], before, AX_X, ALU.add))
                done(nc.vector.tensor_tensor(end[:, :], start[:, :], tiles[:, :], ALU.add))
                per_slot = slots[:, :].unsqueeze(2).broadcast_to([P, NSL, NE])
                done(nc.vector.tensor_tensor(ended, end[:, :].unsqueeze(1).broadcast_to([P, NSL, NE]), per_slot, ALU.is_le))
                nc.vector.tensor_tensor(begun, start[:, :].unsqueeze(1).broadcast_to([P, NSL, NE]), per_slot,
                                        ALU.is_le).then_inc(route_step, 1)
                done(nc.vector.scalar_tensor_tensor(out=where, in0=start[:, :].unsqueeze(1).broadcast_to([P, NSL, NE]),
                                                    scalar=-float(P), in1=where0[:, :, :], op0=ALU.mult, op1=ALU.add))
                step[0] += 1
                dve.wait_ge(route_step, step[0])
                done(nc.vector.tensor_tensor(begun, begun, ended, ALU.subtract))
                done(nc.vector.tensor_tensor(where, where, begun, ALU.mult))
                done(nc.vector.tensor_reduce(slot_f[:, :], where, AX_X, ALU.add))
                nc.vector.tensor_scalar(slot_row[:, :], slot_f[:, :], float(EMPTY0), None, ALU.add).then_inc(slot_row_ready, 1)
                dve.wait_ge(slot_row_ready, 1)
                done(nc.vector.tensor_reduce(slot_f[:, :], ended, AX_X, ALU.add))
                nc.vector.tensor_scalar(slot_off[:, :], slot_f[:, :], float(NE - 1), float(O), ALU.min,
                                        ALU.mult).then_inc(slot_off_ready, 1)

            dve.wait_ge(consts_ready, 16)
            dve.wait_ge(w_ready, 4)

            def step(s, u):
                if not below(s, 2):
                    choose(s - 2)
                if not below(s, 1):
                    y2T_low(s - 1, 1 - u)
                residual(s, u)
                residual_scale(s, u)

            step(0, 0)
            for s in (1, 2, 3):
                for n in range((s - 1) * 3, min(s * 3, WU)):
                    weight_lo(n)
                if s == 2:
                    folded_bias()
                step(s, s % 2)
            with dve.Fori(2, NT // 2) as h:
                step(2 * h, 0)
                step(2 * h + 1, 1)
            choose(NT - 2)
            fold_lo_part(0)
            y2T_low(NT - 1, 1)
            for n in range(1, NU):
                if n + WU - 1 < NU:
                    weight_lo(n + WU - 1)
                fold_lo_part(n)
                if n == 1:
                    choose(NT - 1)
                if n == 3:
                    place_add(NT - 1)
                    place_mask(NT - 1)
                    place_sum(NT - 1)
                    route()

            def slot_norm(s):
                dve.wait_ge(slot_loaded[s], 16)
                if s >= 4:
                    dve.wait_ge(zT_ready, s - 3)
                nc.vector.tensor_scalar(y2[:, s % 4, :], srt[:, s, 0:D], srt[:, s, R_RS:R_RS + 1], srt[:, s, R_NMR:R_NMR + 1],
                                        ALU.mult, ALU.add).then_inc(z_dve, 1)

            def slot_lo(s):
                dve.wait_ge(zT_hi_done, s + 1)
                nc.vector.tensor_tensor(y2T[:, s % 4, 1, :, :], ps[:, T_BANKS[s % 2], 0:D].rearrange("p (k t) -> p k t", k=KD),
                                        y2T[:, s % 4, 0, :, :], ALU.subtract).then_inc(zT_lo_done, 1)

            def slot_sum(s):
                dve.wait_ge(o_ready, s + 1)
                if s % 2 == 0:
                    dve.wait_ge(z_act, s // 2 + 1)
                nc.vector.scalar_tensor_tensor(out=srt[:, s, 0:D], in0=ps[:, C_BANKS[s % 2], 0:O], scalar=OUT_UNSCALE,
                                               in1=srt[:, s, 0:D], op0=ALU.mult, op1=ALU.add).then_inc(o_done, 1)

            slot_norm(1)
            for s in range(NSL):
                slot_lo(s)
                if s % 2 == 0 and s + 3 < NSL:
                    slot_norm(s + 3)
                if s:
                    slot_sum(s - 1)
            slot_sum(NSL - 1)

        @block.tensor
        def _(pe):
            def transposes(n):
                bank = ps[:, 6 + n % 2, :]
                if n >= 2:
                    pe.wait_ge(tr_hi_done, n - 1)
                    pe.wait_ge(tr_lo_done, n - 1)
                g = n // 2
                if n % 2 == 0:
                    pe.wait_ge(y_act, 2 * g + 2)
                else:
                    pe.wait_ge(y_dve, g + 1)
                    pe.wait_ge(y_pool, g + 1)
                for k in range(KD):
                    for h in range(2):
                        ins = nc.tensor.transpose(bank[:, (2 * k + h) * P:(2 * k + h + 1) * P],
                                                  ynorm[:, 2 * n + h, k * P:(k + 1) * P], ident[:, :])
                ins.then_inc(tr_ready, 1)

            def score_products(j, b, r, chunks):
                for k in range(KD):
                    for part, others in ((cT_hi, (yT_hi, yT_lo)), (cT_lo, (yT_hi,))):
                        w = part[:, bass.ds(j, 1), :].rearrange("p a d -> p (a d)")[:, k * P:k * P + r]
                        for other in others:
                            for c in chunks:
                                first = k == 0 and part is cT_hi and other is yT_hi
                                last = k == KD - 1 and part is cT_lo
                                ins = nc.tensor.matmul(ps[0:r, 4 * b + c, :], w, other[:, k, c * BANK:(c + 1) * BANK],
                                                       start=first, stop=last)
                return ins

            def scores(j, b, r):
                pe.wait_ge(cT_ready, j + 1)
                if not below(j, 2):
                    pe.wait_ge(exp_done, j - 1)
                score_products(j, b, r, range(NC)).then_inc(scores_ready, 1)

            def first_scores(j, c):
                pe.wait_ge(tr_hi_done, NG if j == 1 and c >= 2 else 2 * c + 2)
                pe.wait_ge(tr_lo_done, NG if j == 1 and c >= 2 else 2 * c + 2)
                pe.wait_ge(cT_ready, j + 1)
                ins = score_products(j, j, P, [c])
                if c == NC - 1:
                    ins.then_inc(scores_ready, 1)

            pe.wait_ge(ident_ready, 1)
            transposes(0)
            transposes(1)
            for c in (0, 1):
                transposes(2 * c + 2)
                transposes(2 * c + 3)
                first_scores(0, c)
                first_scores(1, c)
            transposes(6)
            transposes(7)
            first_scores(0, 2)
            first_scores(0, 3)
            first_scores(1, 2)
            first_scores(1, 3)
            with pe.Fori(1, NF // 2) as h:
                scores(2 * h, 0, P)
                scores(2 * h + 1, 1, P)
            scores(NF, 0, REST)

            def fold_products(n):
                pe.wait_ge(wT_lo_done, n + 1)
                if n >= 2:
                    pe.wait_ge(fold_lo_done, n - 1)
                m = 0
                for c in range(KH):
                    for part, other in ((0, ow_hi), (0, ow_lo), (1, ow_hi)):
                        ins = nc.tensor.matmul(ps[:, FOLD_BANKS[n % 2], 0:O], wT[:, n % WU, part, c, :], other[:, c, :],
                                               start=m == 0, stop=m == 3 * KH - 1)
                        m += 1
                ins.then_inc(fold_ready, 1)

            def bias_products():
                m = 0
                for c in range(KH):
                    for part, other in ((eb_hi, ow_hi), (eb_hi, ow_lo), (eb_lo, ow_hi)):
                        ins = nc.tensor.matmul(ps[0:NE, R_BANK, 0:O], part[:, c, :], other[:, c, :],
                                               start=m == 0, stop=m == 3 * KH - 1)
                        m += 1
                ins.then_inc(bias_acc, 1)

            def attend(i, b, tiles):
                if 0 in tiles and not below(i, 2):
                    pe.wait_ge(x1_done, i - 1)
                for j in tiles:
                    r = P if j < NF else REST
                    for m, (left, right) in enumerate(((p_hi, ctxn_hi), (p_hi, ctxn_lo), (p_lo, ctxn_hi))):
                        ins = nc.tensor.matmul(ps[:, C_BANKS[b], 0:D], left[0:r, j, bass.ds(i * P, P)], right[0:r, j, :],
                                               start=j == 0 and m == 0, stop=j == NS - 1 and m == 2)
                if NS - 1 in tiles:
                    ins.then_inc(c_ready, 1)

            def y2_transposes(i, b):
                pe.wait_ge(y2_ready, i + 1)
                if not below(i, 1):
                    pe.wait_ge(y2T_lo_done, i)
                for k in range(KD):
                    ins = nc.tensor.transpose(ps[:, T_BANKS[0], k * P:(k + 1) * P], y2[:, b, k * P:(k + 1) * P], ident[:, :])
                ins.then_inc(y2T_ready, 1)

            def logits(i, b):
                pe.wait_ge(y2T_lo_done, i + 1)
                if not below(i, 1):
                    pe.wait_ge(lg_done, i)
                m = 0
                for k in range(KD):
                    for part, other in ((0, gw_hi), (0, gw_lo), (1, gw_hi)):
                        ins = nc.tensor.matmul(logits_ps, y2T[:, b, part, k, :], other[:, k, :], start=m == 0, stop=m == 3 * KD - 1)
                        m += 1
                ins.then_inc(logits_ready, 1)

            def ranks(i):
                pe.wait_ge(seen_ready, i + 1)
                if not below(i, 1):
                    pe.wait_ge(place_added, i)
                else:
                    pe.wait_ge(bias_step, 1)
                nc.tensor.matmul(rank_ps, lower16[:, :], onehot[:, bass.ds(i, 1), :].rearrange("p a e -> p (a e)"),
                                 start=True, stop=False)
                nc.tensor.matmul(rank_ps, ones16[:, :], seen[:, bass.ds(i, 1), :].rearrange("p a e -> p (a e)"),
                                 start=False, stop=True).then_inc(rank_ready, 1)

            def counts():
                pe.wait_ge(place_added, NT)
                nc.tensor.matmul(count_ps, ones16[:, :], seen[:, NT, :], start=True, stop=True).then_inc(counts_ready, 1)

            EARLY = NF - 1
            pe.wait_ge(exp_done, NF)
            pe.wait_ge(w_ready, 4)
            bias_products()
            pe.wait_ge(p_lo_ready, EARLY)
            pe.wait_ge(p_lo_pool_ready, EARLY)
            pe.wait_ge(ctxn_ready, EARLY)
            attend(0, 0, range(EARLY))
            attend(1, 1, range(EARLY))
            pe.wait_ge(p_lo_ready, NS)
            pe.wait_ge(p_lo_pool_ready, NS)
            pe.wait_ge(ctxn_ready, NS)
            attend(0, 0, range(EARLY, NS))
            attend(1, 1, range(EARLY, NS))

            def step(s, u):
                attend(s, u, range(4))
                logits(s - 2, u)
                attend(s, u, range(4, 10))
                y2_transposes(s - 1, 1 - u)
                attend(s, u, range(10, NS))
                ranks(s - 2)

            y2_transposes(0, 0)
            step(2, 0)
            step(3, 1)
            with pe.Fori(2, NT // 2) as h:
                step(2 * h, 0)
                step(2 * h + 1, 1)
            fold_products(0)
            logits(NT - 2, 0)
            fold_products(1)
            y2_transposes(NT - 1, 1)
            ranks(NT - 2)
            fold_products(2)
            logits(NT - 1, 1)
            fold_products(3)
            ranks(NT - 1)
            for n in range(4, NU):
                fold_products(n)
                if n == 4:
                    counts()

            pe.wait_ge(fold_hi_done, NU)
            pe.wait_ge(fold_lo_done, NU)
            pe.wait_ge(bias_spread, 32)
            pe.wait_ge(slot_off_ready, 1)

            def slot_transposes(s):
                pe.wait_ge(z_dve if s % 2 else z_act, s // 2 + 1)
                if s >= 2:
                    pe.wait_ge(zT_lo_done, s - 1)
                for k in range(KD):
                    ins = nc.tensor.transpose(ps[:, T_BANKS[s % 2], k * P:(k + 1) * P], y2[:, s % 4, k * P:(k + 1) * P], ident[:, :])
                ins.then_inc(zT_ready, 1)

            def slot_products(s):
                off = nc.tensor.value_load(slot_off[0:1, s:s + 1], min_val=0, max_val=(NE - 1) * O)
                if s >= 2:
                    pe.wait_ge(o_done, s - 1)
                dst = ps[:, C_BANKS[s % 2], 0:O]
                nc.tensor.matmul(dst, ones16[0:2, :], bias2[:, bass.ds(off, O)], start=True, stop=False)
                pe.wait_ge(zT_lo_done, s + 1)
                m = 0
                for k in range(KD):
                    for part, other in ((0, fold_hi), (0, fold_lo), (1, fold_hi)):
                        ins = nc.tensor.matmul(dst, y2T[:, s % 4, part, k, :], other[:, k, bass.ds(off, O)],
                                               start=False, stop=m == 3 * KD - 1)
                        m += 1
                ins.then_inc(o_ready, 1)

            slot_transposes(0)
            for s in range(1, NSL):
                slot_transposes(s)
                slot_products(s - 1)
            slot_products(NSL - 1)


_INS = [('x', None), ('ctx_1024', None), ('ctx_1024', (2, 1, 0)), ('g_xattn', None), ('g_ffn', None), ('L0_ffn_gate_w', None),
        ('L0_ffn_gate_b', None), ('L0_ffn_expert_w', (0, 2, 1)), ('L0_ffn_expert_b', (1, 0)), ('L0_ffn_out_w', None),
        ('L0_ffn_out_b', None)]
_OUTS = [((1, 2048, 256), 'float32')]


def kernel(**inputs):
    import numpy as _np
    import concourse.bacc as _bacc
    from concourse import mybir as _mybir
    from concourse.bass_utils import run_bass_kernel_spmd as _run

    nc = _bacc.Bacc("TRN2", target_bir_lowering=False, num_devices=1)
    arrays, args = {}, []
    for name, order in _INS:
        a = _np.asarray(inputs[name])
        if order is not None:
            a = a.transpose(order)
            name = name + "_t"
        a = _np.ascontiguousarray(a)
        if name == "ctx_1024_t":
            a = a.reshape(a.shape[0:2])
        arrays[f"in_{name}_dram"] = a
        args.append(nc.dram_tensor(f"in_{name}_dram", a.shape, _mybir.dt.from_np(a.dtype), kind="ExternalInput").ap())
    for i, (shape, dtype) in enumerate(_OUTS):
        dt = _mybir.dt.from_np(_np.dtype(dtype))
        args.append(nc.dram_tensor(f"out_{i}_dram", shape, dt, kind="ExternalOutput").ap())
    bass_flamingo_gated_block(nc, *args)
    r = _run(nc, [arrays], core_ids=[0])
    got = tuple(r.results[0][f"out_{i}_dram"] for i in range(len(_OUTS)))
    return got[0]
```

```python
from contextlib import ExitStack

import concourse.bass as bass
from concourse import mybir

ALU = mybir.AluOpType
ACT = mybir.ActivationFunctionType
F32 = mybir.dt.float32
F16 = mybir.dt.float16
I32 = mybir.dt.int32
AX_X = mybir.AxisListType.X

P = 128
BANK = 512

LN2 = 0.6931471805599453
PROB_SHIFT = 10 * LN2
CTX_SCALE = 2.0 ** 16
C_UNSCALE = 2.0 ** -16
W_SCALE = 2.0 ** 8
M_SCALE = 2.0 ** -8
OUT_UNSCALE = 2.0 ** -8
EPS = 1e-5



def bass_flamingo_gated_block(
    nc: bass.Bass,
    x: bass.AP,
    ctx_rows: bass.AP,
    ctx_cols: bass.AP,
    g_xattn: bass.AP,
    g_ffn: bass.AP,
    gate_w: bass.AP,
    gate_b: bass.AP,
    expert_wt: bass.AP,
    expert_bt: bass.AP,
    out_w: bass.AP,
    out_b: bass.AP,
    out: bass.AP,
):
    _, T, D = x.shape
    S = ctx_rows.shape[1]
    NE, H, _ = expert_wt.shape
    O = out_w.shape[1]
    NT = T // P
    NS = -(-S // P)
    NF = S // P
    REST = S - NF * P
    SPARE = P - REST
    LEFT = REST - SPARE
    KD = D // P
    KH = H // P
    NC = T // BANK
    WS = 2
    NU = NE * KD
    WU = 4
    XG = 4
    NX = NT // XG
    POOL_T = T - BANK
    NSL = NT + NE - 1
    ROW = D + 3
    R_RS, R_NMR, R_ID = D, D + 1, D + 2
    ID_BITS = 3
    GROUP = 8
    WORDS = -(-NSL // GROUP)
    NOBODY = 1 << 20
    REGION = P + T
    EMPTY0 = NE * REGION
    assert 0 < LEFT and REST + LEFT <= P
    assert KD == 2 and NC == 4 and NS == NF + 1 and NF % 2 == 0 and D == O == 256 and NE == 1 << ID_BITS

    def below(i, n):
        return isinstance(i, int) and i < n

    with ExitStack() as stack:
        def sb(name, shape, dt):
            return stack.enter_context(nc.sbuf_tensor(name, shape, dt))

        def sem(name):
            return stack.enter_context(nc.semaphore(name))

        xr = sb("xr", [P, NT, ROW], F32)
        xt = xr[:, :, 0:D]
        xr_id = xr[:, :, :].bitcast(I32)[:, :, R_ID]
        ctx = sb("ctx", [P, NS, D], F32)
        prob = sb("prob", [P, 2, T], F32)
        ynorm = prob[:, :, :].rearrange("p b (t d) -> p (b t) d", d=D)
        wT = prob[:, :, :].rearrange("p b t -> p (b t)").bitcast(F16)[:, 0:WU * 2 * KH * P].rearrange(
            "p (u s c d) -> p u s c d", u=WU, s=2, c=KH)
        yT_hi = sb("yT_hi", [P, KD, T], F16)
        yT_lo = sb("yT_lo", [P, KD, T], F16)
        fold_hi, fold_lo = yT_hi, yT_lo
        cT_hi = sb("cT_hi", [P, NS, D], F16)
        cT_lo = sb("cT_lo", [P, NS, D], F16)
        ctxn_hi, ctxn_lo = cT_hi, cT_lo
        p_hi = sb("p_hi", [P, NS, T], F16)
        p_lo = sb("p_lo", [P, NS, T], F16)
        ow = p_lo[:, NF, :].bitcast(F32).rearrange("p (c o) -> p c o", c=KH)
        wT_late = [p[:, NF - KH:NF, :] for p in (p_hi, p_lo)]
        srt = p_lo[:, :, :].rearrange("p j t -> p (j t)")[:, 0:NSL * ROW * 2].bitcast(F32).rearrange("p (s w) -> p s w", w=ROW)
        srt_id = p_lo[:, :, :].rearrange("p j t -> p (j t)")[:, 0:NSL * ROW * 2].bitcast(I32).rearrange("p (s w) -> p s w", w=ROW)
        bias2 = p_hi[0:2, 0, 0:NE * O]
        assert NSL * ROW * 2 <= (NF - KH) * T and NU - WU <= NT and NU == NT
        stage = sb("stage", [P, KD * S], F32)
        ctxT = stage[:, :].rearrange("p (k s) -> p k s", k=KD)
        ew = stage[:, 0:WS * KH * D].rearrange("p (w c d) -> p w c d", w=WS, c=KH)
        late = ctx[:, :, :].rearrange("p j d -> p (j d)")
        y2 = late[:, 0:4 * D].rearrange("p (b d) -> p b d", b=4)
        y2T = late[:, 4 * D:8 * D].bitcast(F16).rearrange("p (b s k t) -> p b s k t", b=4, s=2, k=KD)
        bias_f = late[0:NE, 8 * D:9 * D]
        bias_hl = late[0:NE, 9 * D:10 * D].bitcast(F16).rearrange("e (s o) -> e s o", s=2)
        rest = 10 * D
        full = late[:, rest:rest + NE * NT].rearrange("p (e n) -> p e n", e=NE)
        before = late[:, rest + NE * NT:rest + NE * (NT + NE)].rearrange("p (e f) -> p e f", e=NE)
        rest += NE * (NT + NE)
        ended, begun, where = [late[:, rest + n * NSL * NE:rest + (n + 1) * NSL * NE].rearrange("p (s e) -> p s e", e=NE)
                               for n in range(3)]
        empty = sb("empty", [P, ROW], F32)
        empty_id = empty[:, :].bitcast(I32)[:, R_ID:R_ID + 1]
        ow_hi = sb("ow_hi", [P, KH, O], F16)
        ow_lo = sb("ow_lo", [P, KH, O], F16)
        eb = sb("eb", [P, KH, NE], F32)
        eb_hi = sb("eb_hi", [P, KH, NE], F16)
        eb_lo = sb("eb_lo", [P, KH, NE], F16)
        ob = sb("ob", [NE, O], F32)
        gw = sb("gw", [P, KD, NE], F32)
        gw_hi = sb("gw_hi", [P, KD, NE], F16)
        gw_lo = sb("gw_lo", [P, KD, NE], F16)
        gb = sb("gb", [P, NE], F32)
        gates = sb("gates", [P, 2], F32)
        tgates = sb("tgates", [P, 2], F32)
        gscale = sb("gscale", [P, 3], F32)
        ctxn_rest = sb("ctxn_rest", [P, D], F16)
        ctxn = sb("ctxn", [P, D], F32)
        ident = sb("ident", [P, P], F32)
        ones16 = sb("ones16", [P, P], F16)
        lower16 = sb("lower16", [P, P], F16)
        desc = sb("desc", [P, NE], F32)
        count_i = sb("count_i", [P, NSL], I32)
        first_i = sb("first_i", [P, NE], I32)
        where_i = sb("where_i", [P, NSL, NE], I32)
        first = sb("first", [P, NE], F32)
        where0 = sb("where0", [P, NSL, NE], F32)
        id_unit = sb("id_unit", [P, WORDS, GROUP], F32)
        slots = sb("slots", [P, NSL], F32)
        thr = sb("thr", [P, NT], F32)
        earlier = sb("earlier", [P, NE, NE], F32)
        eps = sb("eps", [P, 1], F32)
        spare = sb("spare", [P, 2], F32)
        held = sb("held", [P, 1], F32)
        stat6 = sb("stat6", [P, NT, 6], F32)
        stat2 = sb("stat2", [P, NT, 2], F32)
        sd = sb("sd", [P, NT], F32)
        rs = sb("rs", [P, NT], F32)
        newt = sb("newt", [P, NT], F32)
        nmr = sb("nmr", [P, NT], F32)
        cmax = sb("cmax", [P, NC], F32)
        smax = sb("smax", [P, NS], F32)
        nbias = sb("nbias", [P, NS], F32)
        zsum = sb("zsum", [P, NS], F32)
        rz = sb("rz", [P, NS], F32)
        bstat6 = sb("bstat6", [P, 2, 6], F32)
        bstat2 = sb("bstat2", [P, 2, 2], F32)
        bsd = sb("bsd", [P, 2], F32)
        lg = sb("lg", [P, NE], F32)
        lmax = sb("lmax", [P, 1], F32)
        wsel = sb("wsel", [P, NE], F32)
        wmax = sb("wmax", [P, 1], F32)
        onehot = sb("onehot", [P, NT, NE], F16)
        seen = sb("seen", [P, NT + 1, NE], F16)
        placing = sb("placing", [P, NE], F32)
        place = sb("place", [P, NT], I32)
        tiles = sb("tiles", [P, NE], F32)
        start = sb("start", [P, NE], F32)
        end = sb("end", [P, NE], F32)
        slot_f = sb("slot_f", [P, NSL], F32)
        slot_id = sb("slot_id", [P, WORDS, GROUP], F32)
        slot_ids = sb("slot_ids", [P, WORDS], I32)
        end_row = sb("end_row", [P, NE], F32)
        slot_row = sb("slot_row", [P, NSL], I32)

        ps = stack.enter_context(nc.psum_tensor("ps", [P, 8, BANK], F32))
        C_BANKS, FOLD_BANKS, T_BANKS, G_BANK, R_BANK, BIAS_BANK = (7, 5), (2, 3, 4, 7), (6, 0), 1, 0, 4
        logits_ps = ps[:, G_BANK, 0:NE]
        rank_ps = ps[:, R_BANK, 0:NE]
        count_ps = ps[:, G_BANK, NE:2 * NE]
        sorted_rows = nc.dram_tensor("sorted_rows", [NE * REGION + P, ROW], F32, kind="Internal").ap()

        def sems(text):
            return [sem(name) for name in text.split()]

        x_first = sem("x_first")
        x_loaded = [sem(f"x_loaded{g}") for g in range(NX)]
        ctxT_loaded = [sem(f"ctxT_loaded{g}") for g in range(3)]
        ew_loaded = [sem(f"ew_loaded{w}") for w in range(WS)]
        slot_loaded = [sem(f"slot_loaded{s}") for s in range(NSL)]
        ctx_loaded, small_loaded, ow_loaded, bias_loaded, bias_spread = sems(
            "ctx_loaded small_loaded ow_loaded bias_loaded bias_spread")
        sorted_out, padded, out_stored = sems("sorted_out padded out_stored")
        ident_zeroed, eps_ready, ident_ready, consts_ready, empty_ready, iota_done = sems(
            "ident_zeroed eps_ready ident_ready consts_ready empty_ready iota_done")
        stat6_done, stat2_done, sd_ready, rs_done, nmr_done, y_act, y_pool = sems(
            "stat6_done stat2_done sd_ready rs_done nmr_done y_act y_pool")
        tr_ready, tr_hi_done, tr_lo_done, cT_hi_done, cT_ready = sems(
            "tr_ready tr_hi_done tr_lo_done cT_hi_done cT_ready")
        tanh_done, gscale_ready, w_scaled, w_hi_done, w_ready = sems("tanh_done gscale_ready w_scaled w_hi_done w_ready")
        chunk_ready, cmax_done = sems("chunk_ready cmax_done")
        scores_ready, smax_done, nbias_ready, exp_done, p_hi_ready, p_lo_ready, p_lo_pool_ready = sems(
            "scores_ready smax_done nbias_ready exp_done p_hi_ready p_lo_ready p_lo_pool_ready")
        rz_ready, ctxn_done, ctxn_hi_done, ctxn_ready = sems("rz_ready ctxn_done ctxn_hi_done ctxn_ready")
        bias_acc, bias_step, rest_ready = sems("bias_acc bias_step rest_ready")
        wT_scaled, wT_hi_done, wT_lo_done, fold_ready, fold_hi_done, fold_lo_done = sems(
            "wT_scaled wT_hi_done wT_lo_done fold_ready fold_hi_done fold_lo_done")
        c_ready, x1_done, b6_done, b2_done, bsd_ready, brs_done, bnmr_ready = sems(
            "c_ready x1_done b6_done b2_done bsd_ready brs_done bnmr_ready")
        y2_ready, y2T_ready, y2T_hi_done, y2T_lo_done = sems("y2_ready y2T_ready y2T_hi_done y2T_lo_done")
        logits_ready, lg_done, lmax_done, wsel_done, wmax_done, onehot_ready, seen_ready = sems(
            "logits_ready lg_done lmax_done wsel_done wmax_done onehot_ready seen_ready")
        rank_ready, place_added, place_masked, place_ready = sems("rank_ready place_added place_masked place_ready")
        counts_ready, route_step, slot_ids_ready, slot_row_ready = sems(
            "counts_ready route_step slot_ids_ready slot_row_ready")
        z_act, z_dve, zT_ready, zT_hi_done, zT_lo_done, o_ready, o_done = sems(
            "z_act z_dve zT_ready zT_hi_done zT_lo_done o_ready o_done")

        x_view = x.rearrange("a (p i) d -> p (a i) d", i=NT)
        out_rows = out.rearrange("a t d -> (a t) d")
        ctx_full = ctx_rows[:, 0:NF * P, :].rearrange("a (j p) d -> p (a j) d", p=P)
        ctx_rest = ctx_rows[0, NF * P:S, :]
        ctxT_view = ctx_cols.rearrange("(k p) s -> p k s", p=P)
        CT_CUTS = (0, 2 * P, 8 * P, S)

        def group_io(n):
            src = ps[:, 6 + n % 2, :].rearrange("p (k c) -> p k c", k=KD)
            return src, [t[:, :, 2 * n * P:2 * (n + 1) * P] for t in (yT_hi, yT_lo)]

        NG = NT // 2

        def weights(n, part):
            return wT[:, n, part, :, :] if below(n, WU) else wT_late[part][:, :, bass.ds((n - WU) * P, P)]

        block = stack.enter_context(nc.Block())

        @block.sync
        def _(sp):
            sp.dma_start(xt[:, 0:2, :], x_view[:, 0:2, :]).then_inc(x_first, 16)
            sp.dma_start(xt[:, 2:XG, :], x_view[:, 2:XG, :]).then_inc(x_loaded[0], 16)
            for g in range(1, NX):
                sp.dma_start(xt[:, XG * g:XG * (g + 1), :], x_view[:, XG * g:XG * (g + 1), :]).then_inc(x_loaded[g], 16)
            for g in range(1, 3):
                a, b = CT_CUTS[g:g + 2]
                sp.dma_start(ctxT[:, :, a:b], ctxT_view[:, :, a:b]).then_inc(ctxT_loaded[g], 16)
            sp.dma_start(gates[:, 0:1], g_xattn.rearrange("(a b) -> a b", a=1).broadcast_to([P, 1])).then_inc(small_loaded, 16)
            sp.dma_start(gates[:, 1:2], g_ffn.rearrange("(a b) -> a b", a=1).broadcast_to([P, 1])).then_inc(small_loaded, 16)
            sp.dma_start(gw[:, :, :], gate_w.rearrange("(k p) e -> p k e", p=P)).then_inc(small_loaded, 16)
            sp.dma_start(gb[:, :], gate_b.rearrange("(a e) -> a e", a=1).broadcast_to([P, NE])).then_inc(small_loaded, 16)
            sp.dma_start(eb[:, :, :], expert_bt.rearrange("(c p) e -> p c e", p=P)).then_inc(small_loaded, 16)
            sp.dma_start(ow, out_w.rearrange("(c p) o -> p c o", p=P)).then_inc(ow_loaded, 16)
            sp.dma_start(ctx[:, 0:NF, :], ctx_full).then_inc(ctx_loaded, 16)
            sp.dma_start(ctx[0:REST, NF, :], ctx_rest).then_inc(ctx_loaded, 16)
            sp.dma_start(ob[:, :], out_b.rearrange("(a o) -> a o", a=1).broadcast_to([NE, O])).then_inc(bias_loaded, 16)
            sp.wait_ge(cT_ready, NS)

            def load_expert(e):
                sp.dma_start(ew[:, e % WS, :, :], expert_wt[e].rearrange("(c p) d -> p c d", p=P)).then_inc(ew_loaded[e % WS], 16)

            for e in range(WS):
                load_expert(e)
            sp.wait_ge(p_hi_ready, NS)
            sp.wait_ge(w_ready, KH)
            sp.dma_start(p_hi[REST:P, NF, :], p_hi[0:SPARE, NF, :]).then_inc(rest_ready, 16)
            sp.dma_start(p_lo[REST:REST + LEFT, NF, :], p_hi[SPARE:REST, NF, :]).then_inc(rest_ready, 16)
            sp.wait_ge(ctxn_ready, NS)
            sp.dma_start(ctxn_hi[REST:P, NF, :], ctxn_lo[0:SPARE, NF, :]).then_inc(rest_ready, 16)
            sp.dma_start(ctxn_rest[0:REST, :], ctxn_hi[0:REST, NF, :]).then_inc(rest_ready, 16)
            sp.dma_start(ctxn_rest[REST:REST + LEFT, :], ctxn_lo[SPARE:REST, NF, :]).then_inc(rest_ready, 16)
            for e in range(WS, NE):
                sp.wait_ge(wT_lo_done, KD * (e - WS + 1))
                load_expert(e)
            sp.wait_ge(empty_ready, 2)
            for e in range(NE + 1):
                sp.dma_start(sorted_rows[e * REGION:e * REGION + P, :], empty[:, :]).then_inc(padded, 16)
            sp.wait_ge(bias_step, 4)
            sp.wait_ge(c_ready, NT)
            for h in range(2):
                sp.dma_start(bias2[h:h + 1, :].rearrange("a (e o) -> a e o", e=NE),
                             bias_hl[:, h, :]).then_inc(bias_spread, 16)
            sp.wait_ge(slot_row_ready, 1)
            sp.wait_ge(sorted_out, 16 * NT)
            sp.wait_ge(padded, 16 * (NE + 1))
            for s in range(NSL):
                row = nc.sync.value_load(slot_row[0:1, s:s + 1], min_val=0, max_val=EMPTY0)
                sp.dma_start(srt[:, s, :], sorted_rows[bass.ds(row, P), :]).then_inc(slot_loaded[s], 16)
            sp.wait_ge(out_stored, 16 * NSL)

        @block.gpsimd
        def _(pool):
            nc.gpsimd.memset(eps[:, :], EPS).then_inc(eps_ready, 1)
            nc.gpsimd.memset(ident[:, :], 0.0).then_inc(ident_zeroed, 1)
            pool.wait_ge(ident_zeroed, 1)
            nc.gpsimd.affine_select(out=ident[:, :], in_=ident[:, :], compare_op=ALU.not_equal, fill=1.0,
                                    base=0, pattern=[[-1, P]], channel_multiplier=1).then_inc(ident_ready, 1)

            def split_columns(j, r):
                hi, lo = [t[:, j, :].rearrange("p (k c) -> p k c", k=KD)[:, :, 0:r] for t in (cT_hi, cT_lo)]
                src = ctxT[:, :, j * P:j * P + r]
                nc.gpsimd.tensor_copy(hi, src).then_inc(cT_hi_done, 1)
                pool.wait_ge(cT_hi_done, j + 1)
                nc.gpsimd.tensor_tensor(lo, src, hi, ALU.subtract).then_inc(cT_ready, 1)

            def norm_tiles(g):
                pool.wait_ge(nmr_done, g + 1)
                for i in range(XG * g + 2, XG * (g + 1)):
                    nc.gpsimd.tensor_scalar(ynorm[:, i, :], xt[:, i, :], rs[:, i:i + 1], nmr[:, i:i + 1],
                                            ALU.mult, ALU.add).then_inc(y_pool, 1)

            pool.wait_ge(ctxT_loaded[0], 16)
            split_columns(0, P)
            norm_tiles(0)
            split_columns(1, P)
            pool.wait_ge(ctxT_loaded[1], 16)
            for g in range(1, NX):
                norm_tiles(g)
                split_columns(g + 1, P)
            for j in range(NX + 1, 8):
                split_columns(j, P)
            pool.wait_ge(ctxT_loaded[2], 16)
            split_columns(8, P)
            split_columns(9, P)

            def normalise_context(j, b, r):
                hi = ctxn_hi[0:r, bass.ds(j, 1), :].rearrange("p a d -> p (a d)")
                lo = ctxn_lo[0:r, bass.ds(j, 1), :].rearrange("p a d -> p (a d)")
                pool.wait_ge(ctxn_done, j + 1)
                nc.gpsimd.tensor_copy(hi, ctxn[0:r, :]).then_inc(ctxn_hi_done, 1)
                pool.wait_ge(ctxn_hi_done, j + 1)
                nc.gpsimd.tensor_tensor(lo, ctxn[0:r, :], hi, ALU.subtract).then_inc(ctxn_ready, 1)
                pool.wait_ge(p_hi_ready, j + 1)
                nc.gpsimd.tensor_tensor(p_lo[0:r, bass.ds(j, 1), POOL_T:T].rearrange("p a t -> p (a t)"), prob[0:r, b, POOL_T:T],
                                        p_hi[0:r, bass.ds(j, 1), POOL_T:T].rearrange("p a t -> p (a t)"),
                                        ALU.subtract).then_inc(p_lo_pool_ready, 1)

            def constants():
                nc.gpsimd.memset(empty[:, :], 0.0).then_inc(empty_ready, 1)
                pool.wait_ge(empty_ready, 1)
                nc.gpsimd.memset(empty_id, NOBODY).then_inc(empty_ready, 1)
                nc.gpsimd.memset(ones16[:, :], 1.0).then_inc(iota_done, 1)
                nc.gpsimd.memset(lower16[:, :], 1.0).then_inc(iota_done, 1)
                nc.gpsimd.memset(earlier[:, :, :], 1.0).then_inc(iota_done, 1)
                nc.gpsimd.iota(count_i[:, :], pattern=[[1, NSL]], base=0, channel_multiplier=0).then_inc(iota_done, 1)
                nc.gpsimd.iota(first_i[:, :], pattern=[[REGION, NE]], base=P, channel_multiplier=0).then_inc(iota_done, 1)
                nc.gpsimd.iota(where_i[:, :, :], pattern=[[-P, NSL], [REGION, NE]], base=-EMPTY0, channel_multiplier=0).then_inc(iota_done, 1)
                pool.wait_ge(iota_done, 6)
                nc.gpsimd.affine_select(out=lower16[:, :], in_=lower16[:, :], compare_op=ALU.is_gt, fill=0.0,
                                        base=0, pattern=[[1, P]], channel_multiplier=-1).then_inc(consts_ready, 1)
                nc.gpsimd.affine_select(out=earlier[:, :, :], in_=earlier[:, :, :], compare_op=ALU.is_gt, fill=0.0,
                                        base=0, pattern=[[1, NE], [-1, NE]], channel_multiplier=0).then_inc(consts_ready, 1)
                nc.gpsimd.tensor_copy(slots[:, :], count_i[:, :]).then_inc(consts_ready, 1)
                nc.gpsimd.tensor_scalar(thr[:, :], count_i[:, 0:NT], float(P), None, ALU.mult).then_inc(consts_ready, 1)
                nc.gpsimd.tensor_copy(first[:, :], first_i[:, :]).then_inc(consts_ready, 1)
                nc.gpsimd.tensor_copy(where0[:, :, :], where_i[:, :, :]).then_inc(consts_ready, 1)
                nc.gpsimd.memset(seen[:, 0, :], 0.0).then_inc(consts_ready, 1)
                for e in range(NE):
                    nc.gpsimd.memset(desc[:, e:e + 1], float(NE - e)).then_inc(consts_ready, 1)
                for n in range(GROUP):
                    nc.gpsimd.memset(id_unit[:, :, n:n + 1], float(1 << ID_BITS * n)).then_inc(consts_ready, 1)
                nc.gpsimd.memset(slot_id[:, :, :], 0.0).then_inc(consts_ready, 1)
                nc.gpsimd.iota(xr_id, pattern=[[1, NT]], base=0, channel_multiplier=NT).then_inc(consts_ready, 1)

            def split_weight(n, whole, hi, lo):
                nc.gpsimd.tensor_scalar(whole, whole, W_SCALE, None, ALU.mult).then_inc(w_scaled, 1)
                pool.wait_ge(w_scaled, n + 1)
                nc.gpsimd.tensor_copy(hi, whole).then_inc(w_hi_done, 1)
                pool.wait_ge(w_hi_done, n + 1)
                nc.gpsimd.tensor_tensor(lo, whole, hi, ALU.subtract).then_inc(w_ready, 1)

            def split_out_w(c):
                split_weight(c, ow[:, c, :], ow_hi[:, c, :], ow_lo[:, c, :])

            pool.wait_ge(ow_loaded, 16)
            split_out_w(0)
            normalise_context(0, 0, P)
            split_out_w(1)
            normalise_context(1, 1, P)
            split_out_w(2)
            normalise_context(2, 0, P)
            normalise_context(3, 1, P)
            split_out_w(3)
            normalise_context(4, 0, P)
            pool.wait_ge(small_loaded, 80)
            split_weight(KH, eb[:, :, :], eb_hi[:, :, :], eb_lo[:, :, :])
            split_weight(KH + 1, gw[:, :, :], gw_hi[:, :, :], gw_lo[:, :, :])
            nc.gpsimd.tensor_scalar(gb[:, :], gb[:, :], W_SCALE, None, ALU.mult).then_inc(w_ready, 1)
            normalise_context(5, 1, P)
            split_columns(10, P)
            normalise_context(6, 0, P)
            split_columns(11, P)
            normalise_context(7, 1, P)
            split_columns(NF, REST)
            with pool.Fori(4, NF // 2) as h:
                normalise_context(2 * h, 0, P)
                normalise_context(2 * h + 1, 1, P)
            normalise_context(NF, 0, REST)
            constants()

            def weight_low(n):
                unit = ew[:, n // KD % WS, :, n % KD * P:(n % KD + 1) * P]
                pool.wait_ge(wT_hi_done, n + 1)
                nc.gpsimd.tensor_scalar(unit, unit, W_SCALE, None, ALU.mult).then_inc(wT_scaled, 1)
                pool.wait_ge(wT_scaled, n + 1)
                nc.gpsimd.tensor_tensor(weights(n, 1), unit, weights(n, 0), ALU.subtract).then_inc(wT_lo_done, 1)

            def scatter(i):
                pool.wait_ge(place_ready, i + 1)
                pool.wait_ge(bnmr_ready, i + 1)
                nc.gpsimd.indirect_dma_start(sorted_rows, bass.IndirectOffsetOnAxis(ap=place[:, i:i + 1], axis=0),
                                             xr[:, i, :], None).then_inc(sorted_out, 16)

            for n in range(NU):
                weight_low(n)
                if n >= 3:
                    scatter(n - 3)
            for i in range(NT - 3, NT):
                scatter(i)
            for s in range(NSL):
                pool.wait_ge(o_done, s + 1)
                nc.gpsimd.indirect_dma_start(out_rows, bass.IndirectOffsetOnAxis(ap=srt_id[:, s, R_ID:R_ID + 1], axis=0),
                                             srt[:, s, 0:D], None, bounds_check=T - 1, oob_is_err=False).then_inc(out_stored, 16)

        @block.scalar
        def _(act):
            act.dma_start(ctxT[:, :, 0:CT_CUTS[1]], ctxT_view[:, :, 0:CT_CUTS[1]]).then_inc(ctxT_loaded[0], 16)
            act.wait_ge(eps_ready, 1)
            nc.scalar.activation(spare[:, 0:1], eps[:, 0:1], ACT.Sqrt)

            def root(g):
                act.wait_ge(stat2_done, XG * (g + 1))
                nc.scalar.activation(sd[:, XG * g:XG * (g + 1)], stat2[:, XG * g:XG * (g + 1), 1], ACT.Sqrt,
                                     bias=eps[:, 0:1]).then_inc(sd_ready, 1)

            def norm_tiles(g):
                act.wait_ge(nmr_done, g + 1)
                for i in range(XG * g, XG * g + 2):
                    nc.scalar.activation(ynorm[:, i, :], xt[:, i, :], ACT.Identity, bias=nmr[:, i:i + 1],
                                         scale=rs[:, i:i + 1]).then_inc(y_act, 1)

            def group_high(n):
                src, (hi, _) = group_io(n)
                act.wait_ge(tr_ready, n + 1)
                nc.scalar.activation(hi, src, ACT.Copy).then_inc(tr_hi_done, 1)

            root(0)
            norm_tiles(0)
            root(1)
            for g in range(NX):
                group_high(2 * g)
                group_high(2 * g + 1)
                if g + 2 < NX:
                    root(g + 2)
                if g + 1 < NX:
                    norm_tiles(g + 1)
            act.wait_ge(small_loaded, 80)
            nc.scalar.activation(tgates[:, :], gates[:, :], ACT.Tanh).then_inc(tanh_done, 1)

            def softmax(j, b, r):
                act.wait_ge(nbias_ready, j + 1)
                if not below(j, 2):
                    act.wait_ge(p_lo_ready, j - 1)
                    act.wait_ge(p_lo_pool_ready, j - 1)
                nc.scalar.activation(prob[0:r, b, :], ps[0:r, 4 * b:4 * b + 4, :].rearrange("p a c -> p (a c)"), ACT.Exp,
                                     bias=nbias[0:r, bass.ds(j, 1)], accum_out=zsum[0:r, bass.ds(j, 1)]).then_inc(exp_done, 1)
                act.wait_ge(exp_done, j + 1)
                nc.scalar.activation(p_hi[0:r, bass.ds(j, 1), :].rearrange("p a t -> p (a t)"), prob[0:r, b, :],
                                     ACT.Copy).then_inc(p_hi_ready, 1)

            softmax(0, 0, P)
            softmax(1, 1, P)
            with act.Fori(1, NF // 2) as h:
                softmax(2 * h, 0, P)
                softmax(2 * h + 1, 1, P)
            act.wait_ge(w_ready, KH)
            softmax(NF, 0, REST)
            nc.scalar.activation(spare[:, 1:2], eps[:, 0:1], ACT.Sqrt)

            def weight_high(n, slot, k, uses):
                act.wait_ge(ew_loaded[slot], 16 * uses)
                if not below(n, WU):
                    act.wait_ge(c_ready, n - WU + 1)
                nc.scalar.activation(weights(n, 0), ew[:, slot, :, k * P:(k + 1) * P], ACT.Copy,
                                     scale=W_SCALE).then_inc(wT_hi_done, 1)

            def fold_hi_copy(n):
                e, k = n // KD, n % KD
                act.wait_ge(fold_ready, n + 1)
                nc.scalar.activation(fold_hi[:, k, e * O:(e + 1) * O], ps[:, FOLD_BANKS[n % 4], 0:O], ACT.Copy,
                                     scale=gscale[:, 1:2]).then_inc(fold_hi_done, 1)

            def y2T_out(i, b):
                act.wait_ge(y2T_ready, i + 1)
                if not below(i, 2):
                    act.wait_ge(logits_ready, i - 1)
                nc.scalar.activation(y2T[:, b, 0, :, :], ps[:, T_BANKS[0], 0:D].rearrange("p (k t) -> p k t", k=KD),
                                     ACT.Copy).then_inc(y2T_hi_done, 1)

            def norm2(i, b):
                act.wait_ge(b2_done, i + 1)
                nc.scalar.activation(bsd[:, b:b + 1], bstat2[:, b, 1:2], ACT.Sqrt, bias=eps[:, 0:1]).then_inc(bsd_ready, 1)
                act.wait_ge(bnmr_ready, i + 1)
                if not below(i, 2):
                    act.wait_ge(y2T_ready, i - 1)
                row = xr[:, bass.ds(i, 1), :].rearrange("p a d -> p (a d)")
                nc.scalar.activation(y2[:, b, :], row[:, 0:D], ACT.Identity, bias=row[:, R_NMR:R_NMR + 1],
                                     scale=row[:, R_RS:R_RS + 1]).then_inc(y2_ready, 1)

            def slot_norm(s):
                act.wait_ge(slot_loaded[s], 16)
                if s >= 4:
                    act.wait_ge(zT_ready, s - 3)
                nc.scalar.activation(y2[:, s % 4, :], srt[:, s, 0:D], ACT.Identity, bias=srt[:, s, R_NMR:R_NMR + 1],
                                     scale=srt[:, s, R_RS:R_RS + 1]).then_inc(z_act, 1)

            def slot_hi(s):
                act.wait_ge(zT_ready, s + 1)
                if s >= 4:
                    act.wait_ge(o_ready, s - 3)
                nc.scalar.activation(y2T[:, s % 4, 0, :, :], ps[:, T_BANKS[s % 2], 0:D].rearrange("p (k t) -> p k t", k=KD),
                                     ACT.Copy).then_inc(zT_hi_done, 1)

            act.wait_ge(ctxn_done, NS)
            act.wait_ge(p_lo_ready, NS)
            act.wait_ge(p_lo_pool_ready, NS)
            def step(s, u):
                y2T_out(s - 1, 1 - u)
                norm2(s, u)

            norm2(0, 0)
            norm2(1, 1)
            y2T_out(0, 0)
            weight_high(0, 0, 0, 1)
            weight_high(1, 0, 1, 1)
            step(2, 0)
            weight_high(2, 1, 0, 1)
            step(3, 1)
            weight_high(3, 1, 1, 1)
            with act.Fori(1, NT // 4) as h:
                for m in range(4):
                    step(4 * h + m, m % 2)
                    weight_high(4 * h + m, m // KD, m % KD, h + 1)
            act.wait_ge(gscale_ready, 3)
            for n in range(3):
                fold_hi_copy(n)
            y2T_out(NT - 1, 1)
            for n in range(3, NU - 2):
                fold_hi_copy(n)
                if 11 <= n < 13:
                    slot_norm(2 * (n - 11))

            slot_hi(0)
            slot_hi(1)
            fold_hi_copy(NU - 2)
            fold_hi_copy(NU - 1)
            slot_norm(4)
            for s in range(2, NSL):
                slot_hi(s)
                if s % 2 == 0 and s + 4 < NSL:
                    slot_norm(s + 4)

        @block.vector
        def _(dve):
            def aggregate(g):
                dve.wait_ge(stat6_done, XG * (g + 1))
                for i in range(XG * g, XG * (g + 1)):
                    nc.vector.bn_aggr(stat2[:, i, :], stat6[:, i, :]).then_inc(stat2_done, 1)

            def scale(g):
                w = slice(XG * g, XG * (g + 1))
                m = 5 * g

                def statistic(h):
                    if g + 1 < NX:
                        i = XG * (g + 1) + h
                        nc.vector.bn_stats(stat6[:, i, :], xt[:, i, :]).then_inc(stat6_done, 1)

                dve.wait_ge(sd_ready, g + 1)
                nc.vector.reciprocal(rs[:, w], sd[:, w]).then_inc(rs_done, 1)
                if g + 1 < NX:
                    dve.wait_ge(x_loaded[g + 1], 16)
                statistic(0)
                dve.wait_ge(rs_done, m + 1)
                nc.vector.tensor_tensor(newt[:, w], rs[:, w], rs[:, w], ALU.mult).then_inc(rs_done, 1)
                statistic(1)
                dve.wait_ge(rs_done, m + 2)
                nc.vector.scalar_tensor_tensor(out=newt[:, w], in0=stat2[:, w, 1], scalar=EPS, in1=newt[:, w],
                                               op0=ALU.add, op1=ALU.mult).then_inc(rs_done, 1)
                statistic(2)
                dve.wait_ge(rs_done, m + 3)
                nc.vector.tensor_scalar(newt[:, w], newt[:, w], -0.5, 1.5, ALU.mult, ALU.add).then_inc(rs_done, 1)
                statistic(3)
                dve.wait_ge(rs_done, m + 4)
                nc.vector.tensor_tensor(rs[:, w], rs[:, w], newt[:, w], ALU.mult).then_inc(rs_done, 1)
                if g + 1 < NX:
                    aggregate(g + 1)
                dve.wait_ge(rs_done, m + 5)
                nc.vector.scalar_tensor_tensor(out=nmr[:, w], in0=stat2[:, w, 0], scalar=-1.0, in1=rs[:, w],
                                               op0=ALU.mult, op1=ALU.mult).then_inc(nmr_done, 1)

            def group_low(n):
                src, (hi, lo) = group_io(n)
                dve.wait_ge(tr_hi_done, n + 1)
                nc.vector.tensor_tensor(lo, src, hi, ALU.subtract).then_inc(tr_lo_done, 1)

            dve.wait_ge(x_first, 16)
            for i in range(XG):
                if i == 2:
                    dve.wait_ge(x_loaded[0], 16)
                nc.vector.bn_stats(stat6[:, i, :], xt[:, i, :]).then_inc(stat6_done, 1)
            aggregate(0)
            for g in range(NX):
                scale(g)
                if g:
                    group_low(2 * g - 2)
                    group_low(2 * g - 1)
            def chunk_max(c):
                dve.wait_ge(chunk_ready, c + 1)
                nc.vector.tensor_reduce(cmax[:, c:c + 1], ps[:, c, :], AX_X, ALU.max).then_inc(cmax_done, 1)

            chunk_max(0)
            chunk_max(1)
            group_low(NG - 2)
            group_low(NG - 1)
            chunk_max(2)
            chunk_max(3)
            dve.wait_ge(cmax_done, NC)
            nc.vector.tensor_reduce(smax[:, 0:1], cmax[:, :], AX_X, ALU.max).then_inc(smax_done, 1)
            dve.wait_ge(smax_done, 1)
            nc.vector.tensor_scalar(nbias[:, 0:1], smax[:, 0:1], -1.0, PROB_SHIFT, ALU.mult, ALU.add).then_inc(nbias_ready, 1)

            dve.wait_ge(tanh_done, 1)
            for n, (col, scale) in enumerate(((0, CTX_SCALE), (1, M_SCALE), (1, W_SCALE))):
                nc.vector.tensor_scalar(gscale[:, n:n + 1], tgates[:, col:col + 1], scale, None, ALU.mult).then_inc(gscale_ready, 1)

            def row_max(j, b, r):
                dve.wait_ge(scores_ready, j)
                c = bass.ds(j, 1)
                nc.vector.tensor_reduce(smax[0:r, c], ps[0:r, 4 * b:4 * b + 4, :].rearrange("p a c -> p (a c)"), AX_X,
                                        ALU.max).then_inc(smax_done, 1)
                dve.wait_ge(smax_done, j + 1)
                nc.vector.tensor_scalar(nbias[0:r, c], smax[0:r, c], -1.0, PROB_SHIFT, ALU.mult, ALU.add).then_inc(nbias_ready, 1)

            def split_prob(j, b, r):
                c = bass.ds(j, 1)
                dve.wait_ge(exp_done, j + 1)
                nc.vector.reciprocal(rz[0:r, c], zsum[0:r, c]).then_inc(rz_ready, 1)
                dve.wait_ge(rz_ready, j + 1)
                if not below(j, 1):
                    dve.wait_ge(ctxn_ready, j)
                nc.vector.tensor_scalar(ctxn[0:r, :], ctx[0:r, c, :].rearrange("p a d -> p (a d)"), rz[0:r, c],
                                        gscale[0:r, 0:1], ALU.mult, ALU.mult).then_inc(ctxn_done, 1)
                dve.wait_ge(p_hi_ready, j + 1)
                nc.vector.tensor_tensor(p_lo[0:r, c, 0:POOL_T].rearrange("p a t -> p (a t)"), prob[0:r, b, 0:POOL_T],
                                        p_hi[0:r, c, 0:POOL_T].rearrange("p a t -> p (a t)"), ALU.subtract).then_inc(p_lo_ready, 1)

            row_max(1, 1, P)
            dve.wait_ge(gscale_ready, 3)
            dve.wait_ge(ctx_loaded, 32)
            split_prob(0, 0, P)
            with dve.Fori(1, NF // 2) as h:
                j = 2 * h
                row_max(j, 0, P)
                split_prob(j - 1, 1, P)
                row_max(j + 1, 1, P)
                split_prob(j, 0, P)
            row_max(NF, 0, REST)
            split_prob(NF - 1, 1, P)
            split_prob(NF, 0, REST)

            def fold_lo_part(n):
                e, k = n // KD, n % KD
                dve.wait_ge(fold_hi_done, n + 1)
                w = slice(e * O, (e + 1) * O)
                nc.vector.scalar_tensor_tensor(out=fold_lo[:, k, w], in0=ps[:, FOLD_BANKS[n % 4], 0:O], scalar=gscale[:, 1:2],
                                               in1=fold_hi[:, k, w], op0=ALU.mult, op1=ALU.subtract).then_inc(fold_lo_done, 1)

            def folded_bias():
                dve.wait_ge(ctxn_done, NS)
                dve.wait_ge(bias_acc, 1)
                dve.wait_ge(bias_loaded, 16)
                nc.vector.scalar_tensor_tensor(out=bias_f, in0=ps[0:NE, BIAS_BANK, 0:O], scalar=C_UNSCALE, in1=ob[:, :],
                                               op0=ALU.mult, op1=ALU.add).then_inc(bias_step, 1)
                dve.wait_ge(bias_step, 1)
                nc.vector.tensor_scalar(bias_f, bias_f, gscale[0:NE, 2:3], None, ALU.mult).then_inc(bias_step, 1)
                dve.wait_ge(bias_step, 2)
                nc.vector.tensor_copy(bias_hl[:, 0, :], bias_f).then_inc(bias_step, 1)
                dve.wait_ge(bias_step, 3)
                nc.vector.tensor_tensor(bias_hl[:, 1, :], bias_f, bias_hl[:, 0, :], ALU.subtract).then_inc(bias_step, 1)

            def choose(i):
                last = not below(i, 1)
                dve.wait_ge(logits_ready, i + 1)
                nc.vector.tensor_tensor(lg[:, :], logits_ps, gb[:, :], ALU.add).then_inc(lg_done, 1)
                if last:
                    place_add(i - 1)
                dve.wait_ge(lg_done, i + 1)
                nc.vector.tensor_reduce(lmax[:, :], lg[:, :], AX_X, ALU.max).then_inc(lmax_done, 1)
                if last:
                    place_mask(i - 1)
                dve.wait_ge(lmax_done, i + 1)
                nc.vector.scalar_tensor_tensor(out=wsel[:, :], in0=lg[:, :], scalar=lmax[:, 0:1], in1=desc[:, :],
                                               op0=ALU.is_equal, op1=ALU.mult).then_inc(wsel_done, 1)
                if last:
                    place_sum(i - 1)
                dve.wait_ge(wsel_done, i + 1)
                nc.vector.tensor_reduce(wmax[:, :], wsel[:, :], AX_X, ALU.max).then_inc(wmax_done, 1)
                dve.wait_ge(wmax_done, i + 1)
                nc.vector.tensor_scalar(onehot[:, bass.ds(i, 1), :].rearrange("p a e -> p (a e)"), wsel[:, :], wmax[:, 0:1],
                                        None, ALU.is_equal).then_inc(onehot_ready, 1)
                dve.wait_ge(onehot_ready, i + 1)
                nc.vector.tensor_tensor(seen[:, bass.ds(i + 1, 1), :], seen[:, bass.ds(i, 1), :], onehot[:, bass.ds(i, 1), :],
                                        ALU.add).then_inc(seen_ready, 1)

            def place_add(i):
                dve.wait_ge(rank_ready, i + 1)
                nc.vector.tensor_tensor(placing[:, :], rank_ps, first[:, :], ALU.add).then_inc(place_added, 1)

            def place_mask(i):
                dve.wait_ge(place_added, i + 1)
                nc.vector.tensor_tensor(placing[:, :], placing[:, :], onehot[:, bass.ds(i, 1), :].rearrange("p a e -> p (a e)"),
                                        ALU.mult).then_inc(place_masked, 1)

            def place_sum(i):
                dve.wait_ge(place_masked, i + 1)
                with nc.allow_low_precision(reason="small whole numbers"):
                    nc.vector.tensor_reduce(place[:, bass.ds(i, 1)], placing[:, :], AX_X, ALU.add).then_inc(place_ready, 1)

            def residual(i, b):
                row = xr[:, bass.ds(i, 1), :].rearrange("p a d -> p (a d)")
                dve.wait_ge(c_ready, i + 1)
                nc.vector.scalar_tensor_tensor(out=row[:, 0:D], in0=ps[:, C_BANKS[b], 0:D], scalar=C_UNSCALE, in1=row[:, 0:D],
                                               op0=ALU.mult, op1=ALU.add).then_inc(x1_done, 1)
                dve.wait_ge(x1_done, i + 1)
                nc.vector.memset(held[:, :], 0.0)
                nc.vector.bn_stats(bstat6[:, b, :], row[:, 0:D]).then_inc(b6_done, 1)
                dve.wait_ge(b6_done, i + 1)
                nc.vector.memset(held[:, :], 0.0)
                nc.vector.bn_aggr(bstat2[:, b, :], bstat6[:, b, :]).then_inc(b2_done, 1)

            def residual_scale(i, b):
                row = xr[:, bass.ds(i, 1), :].rearrange("p a d -> p (a d)")
                dve.wait_ge(bsd_ready, i + 1)
                nc.vector.reciprocal(row[:, R_RS:R_RS + 1], bsd[:, b:b + 1]).then_inc(brs_done, 1)
                dve.wait_ge(brs_done, i + 1)
                nc.vector.scalar_tensor_tensor(out=row[:, R_NMR:R_NMR + 1], in0=bstat2[:, b, 0:1], scalar=-1.0,
                                               in1=row[:, R_RS:R_RS + 1], op0=ALU.mult, op1=ALU.mult).then_inc(bnmr_ready, 1)

            def y2T_low(i, b):
                dve.wait_ge(y2T_hi_done, i + 1)
                nc.vector.tensor_tensor(y2T[:, b, 1, :, :], ps[:, T_BANKS[0], 0:D].rearrange("p (k t) -> p k t", k=KD),
                                        y2T[:, b, 0, :, :], ALU.subtract).then_inc(y2T_lo_done, 1)

            def route():
                step = [0]

                def done(ins):
                    step[0] += 1
                    ins.then_inc(route_step, 1)

                def wait():
                    dve.wait_ge(route_step, step[0])

                dve.wait_ge(counts_ready, 1)
                done(nc.vector.tensor_tensor(full, count_ps.unsqueeze(2).broadcast_to([P, NE, NT]),
                                             thr[:, :].unsqueeze(1).broadcast_to([P, NE, NT]), ALU.is_gt))
                place_add(NT - 1)
                wait()
                done(nc.vector.tensor_reduce(tiles[:, :], full, AX_X, ALU.add))
                place_mask(NT - 1)
                wait()
                done(nc.vector.tensor_tensor(before, tiles[:, :].unsqueeze(1).broadcast_to([P, NE, NE]), earlier[:, :, :], ALU.mult))
                place_sum(NT - 1)
                wait()
                done(nc.vector.tensor_reduce(start[:, :], before, AX_X, ALU.add))
                wait()
                done(nc.vector.tensor_tensor(end[:, :], start[:, :], tiles[:, :], ALU.add))
                done(nc.vector.scalar_tensor_tensor(out=end_row[:, :], in0=start[:, :], scalar=float(P), in1=count_ps,
                                                    op0=ALU.mult, op1=ALU.add))
                fold_lo_part(5)
                wait()
                per_slot = slots[:, :].unsqueeze(2).broadcast_to([P, NSL, NE])
                done(nc.vector.tensor_tensor(ended, end[:, :].unsqueeze(1).broadcast_to([P, NSL, NE]), per_slot, ALU.is_le))
                done(nc.vector.tensor_tensor(begun, start[:, :].unsqueeze(1).broadcast_to([P, NSL, NE]), per_slot, ALU.is_le))
                done(nc.vector.tensor_tensor(where, end_row[:, :].unsqueeze(1).broadcast_to([P, NSL, NE]), where0[:, :, :], ALU.add))
                wait()
                done(nc.vector.tensor_tensor(begun, begun, ended, ALU.subtract))
                fold_lo_part(6)
                wait()
                done(nc.vector.tensor_tensor(where, where, begun, ALU.mult))
                wait()
                done(nc.vector.tensor_reduce(slot_f[:, :], where, AX_X, ALU.add))
                fold_lo_part(7)
                wait()
                nc.vector.tensor_scalar(slot_row[:, :], slot_f[:, :], float(EMPTY0), None, ALU.add).then_inc(slot_row_ready, 1)
                fold_lo_part(8)
                dve.wait_ge(slot_row_ready, 1)
                done(nc.vector.tensor_reduce(slot_f[:, :], ended, AX_X, ALU.add))
                wait()
                flat = slot_id[:, :, :].rearrange("p g n -> p (g n)")[:, 0:NSL]
                units = id_unit[:, :, :].rearrange("p g n -> p (g n)")[:, 0:NSL]
                done(nc.vector.scalar_tensor_tensor(out=flat, in0=slot_f[:, :], scalar=float(NE - 1), in1=units,
                                                    op0=ALU.min, op1=ALU.mult))
                fold_lo_part(9)
                wait()
                with nc.allow_low_precision(reason="whole numbers of 24 bits"):
                    nc.vector.tensor_reduce(slot_ids[:, :], slot_id[:, :, :], AX_X, ALU.add).then_inc(slot_ids_ready, 1)
                fold_lo_part(10)

            def slot_norm(s):
                dve.wait_ge(slot_loaded[s], 16)
                if s >= 4:
                    dve.wait_ge(zT_ready, s - 3)
                nc.vector.tensor_scalar(y2[:, s % 4, :], srt[:, s, 0:D], srt[:, s, R_RS:R_RS + 1], srt[:, s, R_NMR:R_NMR + 1],
                                        ALU.mult, ALU.add).then_inc(z_dve, 1)

            def slot_lo(s):
                dve.wait_ge(zT_hi_done, s + 1)
                nc.vector.tensor_tensor(y2T[:, s % 4, 1, :, :], ps[:, T_BANKS[s % 2], 0:D].rearrange("p (k t) -> p k t", k=KD),
                                        y2T[:, s % 4, 0, :, :], ALU.subtract).then_inc(zT_lo_done, 1)

            def slot_sum(s):
                dve.wait_ge(o_ready, s + 1)
                if s % 2 == 0:
                    dve.wait_ge(z_act, s // 2 + 1)
                nc.vector.scalar_tensor_tensor(out=srt[:, s, 0:D], in0=ps[:, C_BANKS[s % 2], 0:O], scalar=OUT_UNSCALE,
                                               in1=srt[:, s, 0:D], op0=ALU.mult, op1=ALU.add).then_inc(o_done, 1)


            def step(s, u):
                choose(s - 2)
                y2T_low(s - 1, 1 - u)
                residual(s, u)
                residual_scale(s, u)

            folded_bias()
            residual(0, 0)
            residual_scale(0, 0)
            residual(1, 1)
            residual_scale(1, 1)
            y2T_low(0, 0)
            dve.wait_ge(consts_ready, 8 + NE + GROUP + 1)
            dve.wait_ge(w_ready, KH + 3)
            residual(2, 0)
            residual_scale(2, 0)
            y2T_low(1, 1)
            choose(0)
            step(3, 1)
            with dve.Fori(2, NT // 2) as h:
                step(2 * h, 0)
                step(2 * h + 1, 1)
            choose(NT - 2)
            for n in range(3):
                fold_lo_part(n)
            y2T_low(NT - 1, 1)
            choose(NT - 1)
            fold_lo_part(3)
            fold_lo_part(4)
            route()
            for n in range(11, NU - 2):
                fold_lo_part(n)
                if n < 13:
                    slot_norm(2 * (n - 11) + 1)

            slot_lo(0)
            slot_lo(1)
            fold_lo_part(NU - 2)
            fold_lo_part(NU - 1)
            slot_norm(5)
            slot_lo(2)
            slot_lo(3)
            slot_norm(7)
            for s in range(4, NSL):
                slot_sum(s - 4)
                slot_lo(s)
                if s % 2 == 1 and s + 4 < NSL:
                    slot_norm(s + 4)
            for s in range(NSL - 4, NSL):
                slot_sum(s)

        @block.tensor
        def _(pe):
            def transposes(n):
                bank = ps[:, 6 + n % 2, :]
                if n >= 2:
                    pe.wait_ge(tr_hi_done, n - 1)
                    pe.wait_ge(tr_lo_done, n - 1)
                g = n // 2
                if n % 2 == 0:
                    pe.wait_ge(y_act, 2 * g + 2)
                else:
                    pe.wait_ge(y_pool, 2 * g + 2)
                for k in range(KD):
                    for h in range(2):
                        ins = nc.tensor.transpose(bank[:, (2 * k + h) * P:(2 * k + h + 1) * P],
                                                  ynorm[:, 2 * n + h, k * P:(k + 1) * P], ident[:, :])
                ins.then_inc(tr_ready, 1)

            def score_products(j, b, r, chunks):
                for k in range(KD):
                    for part, others in ((cT_hi, (yT_hi, yT_lo)), (cT_lo, (yT_hi,))):
                        w = part[:, bass.ds(j, 1), :].rearrange("p a d -> p (a d)")[:, k * P:k * P + r]
                        for other in others:
                            for c in chunks:
                                first = k == 0 and part is cT_hi and other is yT_hi
                                last = k == KD - 1 and part is cT_lo
                                ins = nc.tensor.matmul(ps[0:r, 4 * b + c, :], w, other[:, k, c * BANK:(c + 1) * BANK],
                                                       start=first, stop=last)
                return ins

            def scores(j, b, r):
                pe.wait_ge(cT_ready, j + 1)
                pe.wait_ge(exp_done, j - 1)
                score_products(j, b, r, range(NC)).then_inc(scores_ready, 1)

            def first_scores(j, c):
                pe.wait_ge(tr_hi_done, NG if j == 1 and c >= 2 else 2 * c + 2)
                pe.wait_ge(tr_lo_done, NG if j == 1 and c >= 2 else 2 * c + 2)
                pe.wait_ge(cT_ready, j + 1)
                ins = score_products(j, j, P, [c])
                if j == 0:
                    ins.then_inc(chunk_ready, 1)
                elif c == NC - 1:
                    ins.then_inc(scores_ready, 1)

            def keep_warm(n):
                with pe.Fori(0, n // KH):
                    for c in range(KH):
                        nc.tensor.transpose(ps[:, 5, c * P:(c + 1) * P], ident[:, :], ident[:, :])

            pe.wait_ge(ident_ready, 1)
            pe.wait_ge(x_first, 16)
            keep_warm(36)
            transposes(0)
            transposes(1)
            keep_warm(20)
            transposes(2)
            transposes(3)
            first_scores(0, 0)
            first_scores(1, 0)
            transposes(4)
            transposes(5)
            first_scores(0, 1)
            first_scores(1, 1)
            transposes(6)
            transposes(7)
            first_scores(0, 2)
            first_scores(0, 3)
            first_scores(1, 2)
            first_scores(1, 3)
            with pe.Fori(1, NF // 2) as h:
                scores(2 * h, 0, P)
                scores(2 * h + 1, 1, P)
            scores(NF, 0, REST)

            def fold_products(n):
                pe.wait_ge(wT_lo_done, n + 1)
                if n >= 4:
                    pe.wait_ge(fold_lo_done, n - 3)
                m = 0
                for c in range(KH):
                    for part, other in ((0, ow_hi), (0, ow_lo), (1, ow_hi)):
                        ins = nc.tensor.matmul(ps[:, FOLD_BANKS[n % 4], 0:O], weights(n, part)[:, c, :], other[:, c, :],
                                               start=m == 0, stop=m == 3 * KH - 1)
                        m += 1
                ins.then_inc(fold_ready, 1)

            def bias_products():
                m = 0
                for c in range(KH):
                    for part, other in ((eb_hi, ow_hi), (eb_hi, ow_lo), (eb_lo, ow_hi)):
                        ins = nc.tensor.matmul(ps[0:NE, BIAS_BANK, 0:O], part[:, c, :], other[:, c, :],
                                               start=m == 0, stop=m == 3 * KH - 1)
                        m += 1
                ins.then_inc(bias_acc, 1)

            def attend(i, b, tiles):
                if 0 in tiles and not below(i, 2):
                    pe.wait_ge(x1_done, i - 1)
                for j in tiles:
                    r = P if j < NF else REST
                    products = [(p_hi, ctxn_hi[0:r, j, :]), (p_hi, ctxn_lo[0:r, j, :]), (p_lo, ctxn_hi[0:r, j, :])]
                    if j == NF and not below(i, 2):
                        products = [(p_hi, ctxn_hi[:, j, :]), (p_lo, ctxn_rest[0:REST + LEFT, :])]
                    for m, (left, right) in enumerate(products):
                        ins = nc.tensor.matmul(ps[:, C_BANKS[b], 0:D], left[0:right.shape[0], j, bass.ds(i * P, P)], right,
                                               start=j == 0 and m == 0, stop=j == NS - 1 and m == len(products) - 1)
                if NS - 1 in tiles:
                    ins.then_inc(c_ready, 1)

            def y2_transposes(i, b):
                pe.wait_ge(y2_ready, i + 1)
                if not below(i, 1):
                    pe.wait_ge(y2T_lo_done, i)
                for k in range(KD):
                    ins = nc.tensor.transpose(ps[:, T_BANKS[0], k * P:(k + 1) * P], y2[:, b, k * P:(k + 1) * P], ident[:, :])
                ins.then_inc(y2T_ready, 1)

            def logits(i, b):
                pe.wait_ge(y2T_lo_done, i + 1)
                if not below(i, 1):
                    pe.wait_ge(lg_done, i)
                m = 0
                for k in range(KD):
                    for part, other in ((0, gw_hi), (0, gw_lo), (1, gw_hi)):
                        ins = nc.tensor.matmul(logits_ps, y2T[:, b, part, k, :], other[:, k, :], start=m == 0, stop=m == 3 * KD - 1)
                        m += 1
                ins.then_inc(logits_ready, 1)

            def ranks(i):
                pe.wait_ge(seen_ready, i + 1)
                if not below(i, 1):
                    pe.wait_ge(place_added, i)
                nc.tensor.matmul(rank_ps, lower16[:, :], onehot[:, bass.ds(i, 1), :].rearrange("p a e -> p (a e)"),
                                 start=True, stop=False)
                nc.tensor.matmul(rank_ps, ones16[:, :], seen[:, bass.ds(i, 1), :].rearrange("p a e -> p (a e)"),
                                 start=False, stop=True).then_inc(rank_ready, 1)

            def counts():
                pe.wait_ge(seen_ready, NT)
                nc.tensor.matmul(count_ps, ones16[:, :], seen[:, NT, :], start=True, stop=True).then_inc(counts_ready, 1)

            EARLY = NF - 1
            pe.wait_ge(exp_done, NF)
            pe.wait_ge(w_ready, KH + 3)
            bias_products()
            pe.wait_ge(p_lo_ready, EARLY)
            pe.wait_ge(p_lo_pool_ready, EARLY)
            pe.wait_ge(ctxn_ready, EARLY)
            attend(0, 0, range(EARLY))
            attend(1, 1, range(EARLY))
            pe.wait_ge(p_lo_ready, NS)
            pe.wait_ge(p_lo_pool_ready, NS)
            pe.wait_ge(ctxn_ready, NS)
            attend(0, 0, range(EARLY, NS))
            attend(1, 1, range(EARLY, NS))

            def step(s, u):
                attend(s, u, range(4))
                ranks(s - 3)
                logits(s - 2, u)
                attend(s, u, range(4, 10))
                y2_transposes(s - 1, 1 - u)
                attend(s, u, range(10, NS))

            attend(2, 0, range(7))
            y2_transposes(0, 0)
            pe.wait_ge(rest_ready, 80)
            attend(2, 0, range(7, NS))
            logits(0, 0)
            y2_transposes(1, 1)
            attend(3, 1, range(5))
            logits(1, 1)
            attend(3, 1, range(5, 8))
            ranks(0)
            attend(3, 1, range(8, 10))
            y2_transposes(2, 0)
            attend(3, 1, range(10, NS))
            with pe.Fori(1, NT // 4) as h:
                for m in range(4):
                    step(4 * h + m, m % 2)
            fold_products(0)
            ranks(NT - 3)
            logits(NT - 2, 0)
            fold_products(1)
            pe.wait_ge(bias_step, 1)
            fold_products(2)
            y2_transposes(NT - 1, 1)
            ranks(NT - 2)
            pe.wait_ge(x1_done, NT - 1)
            fold_products(3)
            logits(NT - 1, 1)
            fold_products(4)
            fold_products(5)
            ranks(NT - 1)
            counts()
            for n in range(6, NU - 2):
                fold_products(n)

            def slot_transposes(s):
                pe.wait_ge(z_dve if s % 2 else z_act, s // 2 + 1)
                if s >= 2:
                    pe.wait_ge(zT_lo_done, s - 1)
                for k in range(KD):
                    ins = nc.tensor.transpose(ps[:, T_BANKS[s % 2], k * P:(k + 1) * P], y2[:, s % 4, k * P:(k + 1) * P], ident[:, :])
                ins.then_inc(zT_ready, 1)

            def slot_products(s):
                off = ((ids[s // GROUP] >> (ID_BITS * (s % GROUP))) & (NE - 1)) * O
                if s >= 2:
                    pe.wait_ge(o_done, s - 1)
                dst = ps[:, C_BANKS[s % 2], 0:O]
                nc.tensor.matmul(dst, ones16[0:2, :], bias2[:, bass.ds(off, O)], start=True, stop=False)
                pe.wait_ge(zT_lo_done, s + 1)
                m = 0
                for k in range(KD):
                    for part, other in ((0, fold_hi), (0, fold_lo), (1, fold_hi)):
                        ins = nc.tensor.matmul(dst, y2T[:, s % 4, part, k, :], other[:, k, bass.ds(off, O)],
                                               start=False, stop=m == 3 * KD - 1)
                        m += 1
                ins.then_inc(o_ready, 1)

            pe.wait_ge(slot_ids_ready, 1)
            ids = [nc.tensor.value_load(slot_ids[0:1, g:g + 1], min_val=0, max_val=(1 << ID_BITS * GROUP) - 1)
                   for g in range(WORDS)]
            slot_transposes(0)
            slot_transposes(1)
            fold_products(NU - 2)
            fold_products(NU - 1)
            slot_transposes(2)
            slot_transposes(3)
            pe.wait_ge(fold_hi_done, NU)
            pe.wait_ge(fold_lo_done, NU)
            pe.wait_ge(bias_spread, 32)
            for s in range(4, NSL):
                slot_products(s - 4)
                slot_transposes(s)
            for s in range(NSL - 4, NSL):
                slot_products(s)


_INS = [('x', None), ('ctx_1024', None), ('ctx_1024', (2, 1, 0)), ('g_xattn', None), ('g_ffn', None), ('L0_ffn_gate_w', None),
        ('L0_ffn_gate_b', None), ('L0_ffn_expert_w', (0, 2, 1)), ('L0_ffn_expert_b', (1, 0)), ('L0_ffn_out_w', None),
        ('L0_ffn_out_b', None)]
_OUTS = [((1, 2048, 256), 'float32')]


def kernel(**inputs):
    import numpy as _np
    import concourse.bacc as _bacc
    from concourse import mybir as _mybir
    from concourse.bass_utils import run_bass_kernel_spmd as _run

    nc = _bacc.Bacc("TRN2", target_bir_lowering=False, num_devices=1)
    arrays, args = {}, []
    for name, order in _INS:
        a = _np.asarray(inputs[name])
        if order is not None:
            a = a.transpose(order)
            name = name + "_t"
        a = _np.ascontiguousarray(a)
        if name == "ctx_1024_t":
            a = a.reshape(a.shape[0:2])
        arrays[f"in_{name}_dram"] = a
        args.append(nc.dram_tensor(f"in_{name}_dram", a.shape, _mybir.dt.from_np(a.dtype), kind="ExternalInput").ap())
    for i, (shape, dtype) in enumerate(_OUTS):
        dt = _mybir.dt.from_np(_np.dtype(dtype))
        args.append(nc.dram_tensor(f"out_{i}_dram", shape, dt, kind="ExternalOutput").ap())
    bass_flamingo_gated_block(nc, *args)
    r = _run(nc, [arrays], core_ids=[0])
    got = tuple(r.results[0][f"out_{i}_dram"] for i in range(len(_OUTS)))
    return got[0]
```
